# Optimizing a Trainium2 kernel written in Bass

```python
import numpy as np
import jax
import jax.numpy as jnp

def _softmax(x, axis=-1):
    return jax.nn.softmax(x, axis=axis)

def _gelu(x):
    return jax.nn.gelu(x, approximate=True)

def _silu(x):
    return jax.nn.silu(x)

def _sigmoid(x):
    return jax.nn.sigmoid(x)

def _layernorm(x, axis=-1, eps=1e-05):
    m = jnp.mean(x, axis=axis, keepdims=True)
    v = jnp.var(x, axis=axis, keepdims=True)
    return (x - m) / jnp.sqrt(v + eps)

def _scatter_add(tgt, idx, src, axis=0):
    return tgt.at[idx].add(src)

def _segment_sum(src, seg, n):
    return jax.ops.segment_sum(src, seg, n)
kernel_name = 'mk_audio_tower_d1_tok_audfeat256_r4_ce6d4f'

def setup_inputs(seed: int=0):
    np.random.seed(seed)
    _w = jnp.asarray

    def _rec_inputs():
        import jax
        import jax.numpy as jnp
        _rk = jax.random.key(seed)
        x = 7.22013e-05 + 1.00017 * jax.random.normal(jax.random.fold_in(_rk, 1), (8, 750, 64), jnp.float32)
        return x
    x = _rec_inputs()

    def _L0_tok_setup():
        import jax, jax.numpy as jnp
        import numpy as np
        WIN = 9
        key = jax.random.key(seed)
        ks = jax.random.split(key, 4)
        N, L, C, U = (8, 1024, 64, 64)
        x = jax.random.normal(ks[0], (N, L, C), dtype=jnp.float32)
        W_qry = jax.random.normal(ks[1], (C, U), dtype=jnp.float32) * 0.05
        W_key = jax.random.normal(ks[2], (C, U), dtype=jnp.float32) * 0.05
        v = jax.random.normal(ks[3], (U,), dtype=jnp.float32) * 0.05
        b = jnp.zeros((U,), dtype=jnp.float32)
        return {'x': x, 'W_qry': W_qry, 'W_key': W_key, 'v': v, 'b': b}
    _L0_tok_all = _L0_tok_setup()
    _L0_tok_in = {k: v for k, v in _L0_tok_all.items() if k in ('W_qry', 'W_key', 'v', 'b')}
    del _L0_tok_all

    def _L0_attn_setup():
        import jax, jax.numpy as jnp
        import numpy as np
        key = jax.random.key(seed)
        k1, k2 = jax.random.split(key)
        B, N, D = (4, 1024, 64)
        inp = jax.random.normal(k1, (B, N, D), dtype=jnp.float32)
        q_weight = jax.random.normal(k2, (D, D), dtype=jnp.float32)
        return {'input': inp, 'q_weight': q_weight}
    _L0_attn_all = _L0_attn_setup()
    _L0_attn_in = {k: v for k, v in _L0_attn_all.items() if k in ('q_weight',)}
    del _L0_attn_all

    def _L0_ffn_setup():
        import jax, jax.numpy as jnp
        import numpy as np
        D_MODEL = 64
        N_EXPERTS = 16
        HIDDEN = 128
        SCALE = 0.02
        key = jax.random.key(seed)
        ks = jax.random.split(key, 5)
        x = jax.random.normal(ks[0], (4, 2048, D_MODEL), dtype=jnp.float32)
        gate_w = jax.random.normal(ks[1], (D_MODEL, N_EXPERTS), dtype=jnp.float32) * SCALE
        gate_b = jnp.zeros((N_EXPERTS,), dtype=jnp.float32)
        w1 = jax.random.normal(ks[2], (N_EXPERTS, D_MODEL, HIDDEN), dtype=jnp.float32) * SCALE
        w2 = jax.random.normal(ks[3], (N_EXPERTS, D_MODEL, HIDDEN), dtype=jnp.float32) * SCALE
        w3 = jax.random.normal(ks[4], (N_EXPERTS, HIDDEN, D_MODEL), dtype=jnp.float32) * SCALE
        return {'x': x, 'gate_w': gate_w, 'gate_b': gate_b, 'w1': w1, 'w2': w2, 'w3': w3}
    _L0_ffn_all = _L0_ffn_setup()
    _L0_ffn_in = {k: v for k, v in _L0_ffn_all.items() if k in ('gate_w', 'gate_b', 'w1', 'w2', 'w3')}
    del _L0_ffn_all
    return {'x': x, 'L0_tok_W_qry': _L0_tok_in['W_qry'], 'L0_tok_W_key': _L0_tok_in['W_key'], 'L0_tok_v': _L0_tok_in['v'], 'L0_tok_b': _L0_tok_in['b'], 'L0_attn_q_weight': _L0_attn_in['q_weight'], 'L0_ffn_gate_w': _L0_ffn_in['gate_w'], 'L0_ffn_gate_b': _L0_ffn_in['gate_b'], 'L0_ffn_w1': _L0_ffn_in['w1'], 'L0_ffn_w2': _L0_ffn_in['w2'], 'L0_ffn_w3': _L0_ffn_in['w3']}

def reference(x, L0_tok_W_qry, L0_tok_W_key, L0_tok_v, L0_tok_b, L0_attn_q_weight, L0_ffn_gate_w, L0_ffn_gate_b, L0_ffn_w1, L0_ffn_w2, L0_ffn_w3):
    import jax
    import jax.numpy as jnp

    def _L0_tok_ref(x, W_qry, W_key, v, b):
        import jax, jax.numpy as jnp
        import numpy as np
        WIN = 9
        N, L, C = x.shape
        n_w = L - WIN + 1
        idx = jnp.arange(n_w)[:, None] + jnp.arange(WIN)[None, :]
        x_win = x[:, idx]
        x_ctr = x[:, WIN // 2:WIN // 2 + n_w]
        key = jnp.einsum('nwsc,cu->nwsu', x_win, W_key)
        qry = jnp.einsum('nwc,cu->nwu', x_ctr, W_qry)
        score = jnp.einsum('nwsu,u->nws', jnp.tanh(qry[:, :, None, :] + key + b), v)
        weight = jax.nn.softmax(score, axis=2)
        out = jnp.einsum('nwsc,nws->nwc', x_win, weight)
        return out

    def _L0_attn_ref(input, q_weight):
        import jax, jax.numpy as jnp
        import numpy as np
        query = jnp.einsum('bnd,de->bne', input, q_weight)
        att = jax.nn.sigmoid(jnp.einsum('bnd,bmd->bnm', query, input))
        value = jnp.einsum('bnm,bmd->bnd', att, input)
        return value

    def _L0_ffn_ref(x, gate_w, gate_b, w1, w2, w3):
        import jax, jax.numpy as jnp
        import numpy as np
        D_MODEL = 64
        N_EXPERTS = 16
        HIDDEN = 128
        SCALE = 0.02
        n_experts = w1.shape[0]
        logits = jnp.einsum('bsd,de->bse', x, gate_w) + gate_b
        probs = jax.nn.softmax(logits, axis=-1)
        top_probs, top_idx = jax.lax.top_k(probs, 2)
        top_probs = top_probs / jnp.sum(top_probs, axis=-1, keepdims=True)
        dispatch = jnp.sum(jax.nn.one_hot(top_idx, n_experts, dtype=x.dtype) * top_probs[..., None], axis=-2)
        h1 = jnp.einsum('bsd,edh->bseh', x, w1)
        h2 = jnp.einsum('bsd,edh->bseh', x, w2)
        hidden = jax.nn.silu(h1) * h2
        expert_out = jnp.einsum('bseh,eho->bseo', hidden, w3)
        return jnp.einsum('bseo,bse->bso', expert_out, dispatch)
    h = _L0_tok_ref(x, L0_tok_W_qry, L0_tok_W_key, L0_tok_v, L0_tok_b)
    h = h + _L0_attn_ref(_layernorm(h, axis=-1), L0_attn_q_weight)
    h = h + _L0_ffn_ref(_layernorm(h, axis=-1), L0_ffn_gate_w, L0_ffn_gate_b, L0_ffn_w1, L0_ffn_w2, L0_ffn_w3)
    return h

_drawn_inputs = setup_inputs


def setup_inputs(seed=0):
    import zlib

    import numpy as np

    out = dict(_drawn_inputs(seed))
    spreads = {'L0_tok_b': (0.0, 0.647), 'L0_ffn_gate_b': (0.0, 2.0)}
    factors = {'L0_ffn_gate_w': 23.444, 'L0_ffn_w1': 21.492, 'L0_ffn_w2': 8.0, 'L0_ffn_w3': 8.0}
    for name, (base, spread) in spreads.items():
        noise = np.random.default_rng([zlib.crc32(name.encode()), seed]).standard_normal(out[name].shape)
        drawn = base * np.exp(spread * noise) if base else spread * noise
        out[name] = jnp.asarray(drawn.astype(out[name].dtype))
    for name, factor in factors.items():
        out[name] = (out[name] * factor).astype(out[name].dtype)
    return out
```

```python
from contextlib import ExitStack

import concourse.bass as bass
from concourse import mybir

F32 = mybir.dt.float32
F32R = mybir.dt.float32r
ALU = mybir.AluOpType
ACT = mybir.ActivationFunctionType
AX = mybir.AxisListType

NB, L, C = 8, 750, 64
WIN = 9
NW = L - WIN + 1
TW, NT = 108, 7
TL = NW - (NT - 1) * TW
KW = TW + WIN - 1
NPAIR = NB // 2
NWP = NT * TW
HALF = NW // 2
NQ = 372
BK = 4 * TW
SEG = 84
QW = 764
KXW = SEG * WIN
E, HID = 16, 128
TOK = NB * NW
CH, NCH = 496, 12
TOKP = CH * NCH
YT = CH // 4
NPE = E // 2
BIG = 3.0e38
AHEAD, DMA_AHEAD = 1, 16


def tile_n(t):
    return TW if t < NT - 1 else TL


def build(nc, x, wq_tok, wk_tok, v_tok, b_tok, q_weight, gate_w, gate_b, w1, w2, w3, out):
    ctx = ExitStack()
    place = [16512]

    def at(name, shape, dt=F32, offset=None):
        size = 4
        for n in shape[1:]:
            size *= n
        if offset is None:
            offset = place[0]
            place[0] += (size + 31) // 32 * 32
        return nc.alloc_sbuf_tensor_at(name, list(shape), dt, offset=offset)

    ident = at("ident", [128, 128])
    stack2 = at("stack2", [128, C])
    band = at("band", [TW, 13 * WIN])
    wq_bd = at("wq_bd", [128, 128])
    wk_bd = at("wk_bd", [128, 128])
    v_col = at("v_col", [128, 1])
    b_col = at("b_col", [128, 1])
    v_sel = at("v_sel", [128, 3, 32])
    qw_f = at("qw_f", [128, 128])
    qw_r = at("qw_r", [128, 128], F32R)
    gw_f = at("gw_f", [128, E])
    gw_hi = at("gw_hi", [128, E], F32R)
    gw_lo = at("gw_lo", [128, E], F32R)
    gb_row = at("gb_row", [TW, E])
    rank = at("rank", [TW, NT, E])
    neg_half = at("neg_half", [TW, 2 * NT])
    w_f = [at(f"w{k}_f", [128, E * HID]) for k in (1, 2)]
    w_hi = [at(f"w{k}_hi", [128, E, HID], F32R) for k in (1, 2)]
    w_lo = [at(f"w{k}_lo", [128, E, HID], F32R) for k in (1, 2)]
    w3_s = at("w3_s", [HID, E, C])
    h_all = at("h_all", [TW, NB, NT, C])
    xn_all = at("xn_all", [TW, NB, NT, C])

    a_base = place[0]
    xk = at("xk", [KW, NPAIR, NT, 2, C])
    x_t = at("x_t", [128, 2, L])
    qb = at("qb", [128, NPAIR, QW])
    kx = at("kx", [128, NPAIR, KXW])
    sc_s = at("sc_s", [96, NWP])
    wt = at("wt", [TW, 2, NT, WIN])
    wt_max = at("wt_max", [TW, 2 * NT])
    wt_sum = at("wt_sum", [TW, 2 * NT])
    band_a = at("band_a", [TW, 2 * NT, 13 * WIN])
    band_t = at("band_t", [KW, 2 * NT, TW])
    ln_c = at("ln_c", [TW, 2 * NT, C])
    ln_sq = at("ln_sq", [TW, 2 * NT, C])
    ln_s = at("ln_s", [TW, 4, 2 * NT])
    a_end = place[0]
    t_base = place[0]
    th = at("th", [128, 2, WIN * QW])
    t_end = place[0]

    place[0] = a_base
    xs = [at(f"xs{p}", [TW, NT, 2, C]) for p in range(2)]
    k_hi = [at(f"k_hi{p}", [128, NWP], F32R) for p in range(2)]
    k_lo = [at(f"k_lo{p}", [128, NWP], F32R) for p in range(2)]
    q_s = [at(f"q_s{p}", [128, 2 * NQ], F32R) for p in range(2)]
    att = [at(f"att{p}", [TW, 2, NQ]) for p in range(2)]
    o_t = at("o_t", [C, NWP])
    assert place[0] <= t_base
    bn_c = at("bn_c", [TW, NT, C])
    assert place[0] <= a_end
    place[0] = t_base
    x3 = at("x3", [128, TOKP], F32R)
    c_base = place[0]
    h2_s = at("h2_s", [TW, NT, C])
    xn2 = at("xn2", [TW, NT, 2, C])
    x2_s = at("x2_s", [128, NWP], F32R)
    bn_sq = at("bn_sq", [TW, NT, C])
    bn_s = at("bn_s", [TW, 4, NT])
    r_a = at("r_a", [TW, NT, E])
    r_b = at("r_b", [TW, NT, E])
    r_c = at("r_c", [TW, NT, E])
    r_m = at("r_m", [TW, 4, NT])
    logit = at("logit", [TW, NB, NT, E])
    onehot = at("onehot", [TW, NB, NT, E])
    zrow = at("zrow", [E, C])
    disp = at("disp", [TW, NB, NT, E])
    d_sum = at("d_sum", [TW, 2, NB * NT])
    d_t = at("d_t", [NT * E, NB, TW])
    assert place[0] <= t_end
    place[0] = c_base + 0
    prod = [at(f"prod{k}", [HID, CH], offset=c_base + k * 2048) for k in range(4)]
    place[0] = a_base
    sil = [at(f"sil{k}", [HID, CH]) for k in range(2)]
    db = [at(f"db{k}", [128, CH]) for k in range(4)]
    res = [at(f"res{k}", [128, CH]) for k in range(2)]
    acc = at("acc", [128, CH])
    acc_f = at("acc_f", [128, CH])
    h2_c = at("h2_c", [YT, 4, C])
    fin = at("fin", [YT, 4, C])
    assert place[0] <= t_base

    h2_d = nc.dram_tensor("h2_d", [TOKP, C], F32).ap()
    dt_d = nc.dram_tensor("dt_d", [E, TOKP], F32).ap()

    ps = ctx.enter_context(nc.psum_tensor("ps", [128, 8, 512], F32))

    def sem(name):
        return ctx.enter_context(nc.semaphore(name))

    w_loaded, pool_const, dve_const, act_const = sem("w_loaded"), sem("pool_const"), sem("dve_const"), sem("act_const")
    x_loaded = [sem(f"x_loaded{p}") for p in range(NPAIR)]
    xt_ps, xt_sb, q_ps, q_sb, k_ps, k_sb = (sem(n) for n in ("xt_ps", "xt_sb", "q_ps", "q_sb", "k_ps", "k_sb"))
    sum_done, tanh_done, sc_ps, sc_sb, sct_ps, wt_copied = (
        sem(n) for n in ("sum_done", "tanh_done", "sc_ps", "sc_sb", "sct_ps", "wt_copied"))
    shifted, exp_done, wt_ready, band_ready, bt_ps = (
        sem(n) for n in ("shifted", "exp_done", "wt_ready", "band_ready", "bt_ps"))
    bt_act, bt_dve, h_ps, h_sb = (sem(n) for n in ("bt_act", "bt_dve", "h_ps", "h_sb"))
    mean_ready, sq_ready, var_ready, rstd_ready, xn_ready = (
        sem(n) for n in ("mean_ready", "sq_ready", "var_ready", "rstd_ready", "xn_ready"))
    xs_loaded, kt_ps, khi_sb, klo_sb, qq_ps, qhi_sb, qlo_sb = (
        sem(n) for n in ("xs_loaded", "kt_ps", "khi_sb", "klo_sb", "qq_ps", "qhi_sb", "qlo_sb"))
    s_ps, sig_done, av_done, o_sb, ot_ps, h2_ready, h2_stored = (
        sem(n) for n in ("s_ps", "sig_done", "av_done", "o_sb", "ot_ps", "h2_ready", "h2_stored"))
    mean2, sq2, var2, rstd2, xn2_ready, x2t_ps, x2hi_sb, x2_ready, x3_stored = (
        sem(n) for n in ("mean2", "sq2", "var2", "rstd2", "xn2_ready", "x2t_ps", "x2hi_sb", "x2_ready", "x3_stored"))
    gate_ps, gate_sb, b_init, routed, gexp_done, disp_ready, dt_ps, dt_sb, dt_stored = (
        sem(n) for n in ("gate_ps", "gate_sb", "b_init", "routed", "gexp_done", "disp_ready", "dt_ps", "dt_sb",
                         "dt_stored"))
    pad_stored = sem("pad_stored")
    h_ready, sil_done, prod_done, out_done, scale_done, add_done, y_done, fin_done = (
        sem(n) for n in ("h_ready", "sil_done", "prod_done", "out_done", "scale_done", "add_done", "y_done",
                         "fin_done"))
    db_loaded = [sem(f"db_loaded{k}") for k in range(4)]
    h2_loaded, out_stored = sem("h2_loaded"), sem("out_stored")
    dve_step, pool_step = sem("dve_step"), sem("pool_step")

    out_rows = out.rearrange("b n c -> (b n) c")
    N_W_LOADS = 2 * 5 + 2 * 2 + 1 + 2 * 2 * 2 + 1

    block = ctx.enter_context(nc.Block())

    @block.sync
    def _(sp):
        for p in range(NPAIR):
            for b in range(2):
                xb = x[2 * p + b]
                rows = bass.AP(xb.tensor, xb.offset, [[C, KW], [TW * C, NT - 1], [1, C]])
                sp.dma_start(xk[:, p, 0:NT - 1, b, :], rows).then_inc(x_loaded[p], 16)
                sp.dma_start(xk[0:TL + WIN - 1, p, NT - 1, b, :], xb[(NT - 1) * TW:L, :]).then_inc(x_loaded[p], 16)

        def stage_in(b, par):
            sp.wait_ge(xs_loaded, b * 32)
            for k in range(2):
                sp.dma_start(xs[par][:, :, k, :], xn_all[:, bass.ds(b, 1), :, :].rearrange("p a t c -> p (a t) c")
                             ).then_inc(xs_loaded, 16)

        def stage_out(b):
            sp.wait_ge(h2_ready, b + 1)
            rows = h2_d[bass.ds(b * NW, (NT - 1) * TW), :].rearrange("(t p) c -> p t c", p=TW)
            sp.dma_start(rows, h2_s[:, 0:NT - 1, :]).then_inc(h2_stored, 16)
            sp.dma_start(h2_d[bass.ds(b * NW + (NT - 1) * TW, TL), :], h2_s[0:TL, NT - 1, :]).then_inc(h2_stored, 16)
            sp.wait_ge(x2_ready, b + 1)
            sp.dma_start(x3[:, bass.ds(b * NW, NW)].bitcast(F32), x2_s[:, 0:NW].bitcast(F32)).then_inc(x3_stored, 16)

        sp.wait_ge(b_init, 1)
        sp.dma_start(h2_d[TOK:TOKP, :], zrow[0:TOKP - TOK, :]).then_inc(pad_stored, 16)
        sp.dma_start(dt_d[:, TOK:TOKP], zrow[:, 0:TOKP - TOK]).then_inc(pad_stored, 16)
        stage_in(0, 0)
        stage_in(1, 1)
        with sp.Fori(0, 3) as i:
            for par in range(2):
                b = i * 2 + par
                sp.wait_ge(av_done, (b + 1) * NT)
                stage_in(b + 2, par)
                stage_out(b)
        stage_out(NB - 2)
        stage_out(NB - 1)

        for b in range(NB):
            if b % 4 == 0:
                sp.wait_ge(dt_sb, b // 4 + 1)
            for t in range(NT - 1):
                sp.dma_start(dt_d[:, b * NW + t * TW:b * NW + (t + 1) * TW],
                             d_t[t * E:(t + 1) * E, b, :]).then_inc(dt_stored, 16)
            sp.dma_start(dt_d[:, b * NW + (NT - 1) * TW:(b + 1) * NW],
                         d_t[(NT - 1) * E:NT * E, b, 0:TL]).then_inc(dt_stored, 16)

        def load_db(c, p):
            src = dt_d[2 * p:2 * p + 2, bass.ds(c * CH, CH)]
            for k in range(2):
                row = src[k:k + 1, :].broadcast_to([C, CH])
                sp.dma_start(db[p % 4][k * C:(k + 1) * C, :], row).then_inc(db_loaded[p % 4], 16)

        def load_h2(c):
            rows = h2_d[bass.ds(c * CH, CH), :].rearrange("(j p) c -> p j c", p=YT)
            sp.dma_start(h2_c[:, :, :], rows).then_inc(h2_loaded, 16)

        def chunk(c, first):
            for p in range(NPE):
                if not (first and p < 4):
                    sp.wait_ge(scale_done, c * NPE + p - 3)
                load_db(c, p)
                if p == 6 and not first:
                    sp.wait_ge(fin_done, c + AHEAD)
                    sp.dma_start(out_rows[bass.ds((c - 1) * CH, CH), :].rearrange("(j p) c -> p j c", p=YT),
                                 fin[:, :, :]).then_inc(out_stored, 16)
                    load_h2(c)

        sp.wait_ge(dt_stored, NB * NT * 16)
        sp.wait_ge(pad_stored, 32)
        sp.wait_ge(h2_stored, NB * 32 + DMA_AHEAD)
        load_h2(0)
        chunk(0, True)
        with sp.Fori(1, NCH) as c:
            chunk(c, False)
        sp.wait_ge(fin_done, NCH + AHEAD)
        base = (NCH - 1) * CH
        sp.dma_start(out_rows[base:base + 3 * YT, :].rearrange("(j p) c -> p j c", p=YT),
                     fin[:, 0:3, :]).then_inc(out_stored, 16)
        sp.dma_start(out_rows[base + 3 * YT:TOK, :], fin[0:TOK - base - 3 * YT, 3, :]).then_inc(out_stored, 16)
        sp.wait_ge(out_stored, (NCH + 1) * 16 + DMA_AHEAD)

    @block.gpsimd
    def _(pool):
        for s in (bt_ps, h_sb, wt_copied, bt_act, bt_dve, sc_ps,
                  band_ready, ot_ps, x2t_ps, gate_sb, fin_done):
            pool.sem_inc(s, AHEAD)
        for s in (h2_stored, x3_stored, out_stored):
            pool.sem_inc(s, DMA_AHEAD)
        nc.gpsimd.memset(wq_bd[:], 0.0).then_inc(pool_const, 1)
        nc.gpsimd.memset(wk_bd[:], 0.0).then_inc(pool_const, 1)
        nc.gpsimd.memset(ident[:], 0.0).then_inc(pool_const, 1)
        nc.gpsimd.memset(stack2[:], 0.0).then_inc(pool_const, 1)
        nc.gpsimd.memset(band[:], 1.0).then_inc(pool_const, 1)
        nc.gpsimd.memset(neg_half[:], -0.5).then_inc(pool_const, 1)
        pool.wait_ge(pool_const, 6)
        nc.gpsimd.affine_select(out=ident[:], in_=ident[:], compare_op=ALU.not_equal, fill=1.0, base=0,
                                pattern=[[-1, 128]], channel_multiplier=1).then_inc(pool_const, 1)
        nc.gpsimd.affine_select(out=stack2[:], in_=stack2[:], compare_op=ALU.not_equal, fill=1.0, base=0,
                                pattern=[[-1, C]], channel_multiplier=1).then_inc(pool_const, 1)
        nc.gpsimd.affine_select(out=band[:], in_=band[:], compare_op=ALU.is_ge, fill=0.0, base=0,
                                pattern=[[1, 13 * WIN]], channel_multiplier=-1).then_inc(pool_const, 1)
        pool.wait_ge(pool_const, 9)
        nc.gpsimd.affine_select(out=stack2[:], in_=stack2[:], compare_op=ALU.not_equal, fill=1.0, base=-C,
                                pattern=[[-1, C]], channel_multiplier=1).then_inc(pool_const, 1)
        nc.gpsimd.affine_select(out=band[:], in_=band[:], compare_op=ALU.is_ge, fill=0.0, base=WIN - 1,
                                pattern=[[-1, 13 * WIN]], channel_multiplier=1).then_inc(pool_const, 1)

        def norm_a(p):
            h = h_all[:, bass.ds(p * 2, 2), :, :].rearrange("q b t c -> q (b t) c")
            pool.wait_ge(mean_ready, p + 1)
            nc.gpsimd.tensor_tensor(ln_c[:], h, ln_s[:, 0, :].unsqueeze(2).broadcast_to([TW, 2 * NT, C]),
                                    ALU.subtract).then_inc(pool_step, 1)
            pool.wait_ge(pool_step, p + 1)
            nc.gpsimd.tensor_tensor(ln_sq[:], ln_c[:], ln_c[:], ALU.mult).then_inc(sq_ready, 1)
            pool.wait_ge(var_ready, p + 1)
            nc.gpsimd.tensor_tensor(ln_s[:, 3, :], ln_s[:, 2, :], neg_half[:], ALU.pow).then_inc(rstd_ready, 1)

        with pool.Fori(0, NPAIR) as p:
            pool.wait_ge(wt_ready, p + 1)
            pool.wait_ge(bt_ps, p * 4 + AHEAD)
            f = wt[:].rearrange("q b t r -> q (b t) r").unsqueeze(2).broadcast_to([TW, 2 * NT, 13, WIN])
            m = band[:].rearrange("q (u r) -> q u r", r=WIN).unsqueeze(1).broadcast_to([TW, 2 * NT, 13, WIN])
            nc.gpsimd.tensor_tensor(band_a[:].rearrange("q n (u r) -> q n u r", r=WIN), f, m,
                                    ALU.mult).then_inc(band_ready, 1)
            norm_a(p)

        with pool.Fori(0, NB) as b:
            pool.wait_ge(mean2, b + 1)
            nc.gpsimd.tensor_tensor(bn_c[:], h2_s[:], bn_s[:, 0, :].unsqueeze(2).broadcast_to([TW, NT, C]),
                                    ALU.subtract).then_inc(pool_step, 1)
            pool.wait_ge(pool_step, b + NPAIR + 1)
            nc.gpsimd.tensor_tensor(bn_sq[:], bn_c[:], bn_c[:], ALU.mult).then_inc(sq2, 1)
            pool.wait_ge(var2, b + 1)
            nc.gpsimd.tensor_tensor(bn_s[:, 3, :], bn_s[:, 2, :], neg_half[:, 0:NT], ALU.pow).then_inc(rstd2, 1)

        def chunk(c, first):
            for p in range(1, NPE):
                pool.wait_ge(scale_done, c * NPE + p + 1)
                pool.wait_ge(add_done, c * 7 + p - 1)
                if p < NPE - 1:
                    nc.gpsimd.tensor_tensor(acc[:], acc[:], res[p % 2][:], ALU.add).then_inc(add_done, 1)
                else:
                    if not first:
                        pool.wait_ge(y_done, c)
                    nc.gpsimd.tensor_tensor(acc_f[:], acc[:], res[p % 2][:], ALU.add).then_inc(add_done, 1)

        chunk(0, True)
        with pool.Fori(1, NCH) as c:
            chunk(c, False)

    @block.scalar
    def _(act):
        def load(dst, src):
            act.dma_start(dst, src).then_inc(w_loaded, 16)

        def col(v):
            return v.rearrange("(p a) -> p a", a=1)

        for k in range(2):
            half = slice(k * C, (k + 1) * C)
            load(b_col[half, :], col(b_tok))
            load(v_col[half, :], col(v_tok))
            load(qw_f[half, 0:C], q_weight)
            load(qw_f[half, C:128], q_weight)
            load(gw_f[half, :], gate_w)
        act.wait_ge(pool_const, 2)
        for k in range(2):
            half = slice(k * C, (k + 1) * C)
            load(wq_bd[half, half], wq_tok)
            load(wk_bd[half, half], wk_tok)
        load(gb_row[:], gate_b.rearrange("(a e) -> a e", a=1).broadcast_to([TW, E]))
        for k in range(2):
            half = slice(k * C, (k + 1) * C)
            for w, dst in ((w1, w_f[0]), (w2, w_f[1])):
                for e0 in (0, E // 2):
                    load(dst[half, e0 * HID:(e0 + E // 2) * HID].rearrange("d (e h) -> d e h", h=HID),
                         w[e0:e0 + E // 2].rearrange("e d h -> d e h"))
        load(w3_s[:], w3.rearrange("e h o -> h e o"))

        for p in range(NPAIR):
            act.wait_ge(xt_ps, p + 1)
            if p >= 2:
                act.wait_ge(k_ps, p - 1)
            act.copy(x_t[:, p % 2, 0:BK], ps[:, 0, 0:BK])
            act.copy(x_t[:, p % 2, BK:L], ps[:, 1, 0:L - BK]).then_inc(xt_sb, 1)
            act.wait_ge(q_ps, p + 1)
            if p == 0:
                act.wait_ge(dve_const, 1)
                act.wait_ge(w_loaded, N_W_LOADS * 16)
            nc.scalar.activation(qb[:, p, 8:8 + NW].rearrange("q (h n) -> q h n", h=2), ps[:, 2:4, 0:HALF],
                                 ACT.Identity, bias=b_col[:]).then_inc(q_sb, 1)
        act.copy(qw_r[:], qw_f[:]).then_inc(act_const, 1)
        act.copy(gw_hi[:], gw_f[:]).then_inc(act_const, 1)
        for k in range(2):
            act.copy(w_hi[k][:].rearrange("d e h -> d (e h)"), w_f[k][:]).then_inc(act_const, 1)

        def exps(p):
            act.wait_ge(shifted, p + 1)
            nc.scalar.activation(wt[:], wt[:], ACT.Exp).then_inc(exp_done, 1)

        with act.Fori(0, NPAIR) as p:
            for g in range(3):
                act.wait_ge(sum_done, p * 3 + g + 1)
                v = th[:, bass.ds(p % 2, 1), :].rearrange("q a (r n) -> q (a r) n", n=QW)[:, 3 * g:3 * g + 3, 8:8 + NW]
                nc.scalar.activation(v, v, ACT.Tanh).then_inc(tanh_done, 1)
            act.wait_ge(sc_ps, p + 1 + AHEAD)
            act.copy(sc_s[:, 0:NW].rearrange("q (h n) -> q h n", h=2), ps[0:96, 0:2, 0:HALF]).then_inc(sc_sb, 1)
            exps(p)
            for k in range(2):
                act.wait_ge(bt_ps, p * 4 + 2 * k + 1 + AHEAD)
                act.copy(band_t[:, 7 * k:7 * k + 4, :].rearrange("q t n -> q (t n)"),
                         ps[0:KW, 4 + 2 * k, 0:BK]).then_inc(bt_act, 1)
            act.wait_ge(h_ps, p + 1)
            act.copy(h_all[:, bass.ds(p * 2, 2), :, :].rearrange("q b t c -> q b (t c)"),
                     ps[0:TW, 0:2, 0:NT * C]).then_inc(h_sb, 1)

        def key_hi(b, par):
            act.wait_ge(kt_ps, b + 1)
            act.copy(k_hi[par][:, 0:BK], ps[:, 4, 0:BK])
            act.copy(k_hi[par][:, BK:NW], ps[:, 5, 0:NW - BK]).then_inc(khi_sb, 1)

        def query_hi(b, par):
            act.wait_ge(qq_ps, b + 1)
            act.copy(q_s[par][:].rearrange("q (h n) -> q h n", h=2), ps[:, 4:6, 0:NQ]).then_inc(qhi_sb, 1)

        def sigmoid(b, par, j):
            n = (par + j) % 2
            act.wait_ge(s_ps, b * NT + j + 1)
            if j >= 2:
                act.wait_ge(av_done, b * NT + j - 1)
            elif j == 1:
                act.wait_ge(av_done, b * NT)
            else:
                act.wait_ge(sig_done, b * NT)
                act.wait_ge(o_sb, b)
            nc.scalar.activation(att[n][0:tile_n(j)], ps[0:tile_n(j), 2 * n:2 * n + 2, 0:NQ],
                                 ACT.Sigmoid).then_inc(sig_done, 1)

        def x2_hi(b):
            act.wait_ge(x2t_ps, b + 1 + AHEAD)
            act.wait_ge(x3_stored, b * 16 + DMA_AHEAD)
            act.copy(x2_s[:, 0:BK], ps[:, 4, 0:BK])
            act.copy(x2_s[:, BK:NW], ps[:, 5, 0:NW - BK]).then_inc(x2hi_sb, 1)

        def step(b, par, tail, prep):
            sigmoid(b, par, 0)
            if prep:
                key_hi(b + 1, 1 - par)
            sigmoid(b, par, 1)
            sigmoid(b, par, 2)
            sigmoid(b, par, 3)
            if prep:
                query_hi(b + 1, 1 - par)
            sigmoid(b, par, 4)
            sigmoid(b, par, 5)
            if tail:
                x2_hi(b - 1)
            sigmoid(b, par, 6)

        act.wait_ge(b_init, 1)
        key_hi(0, 0)
        query_hi(0, 0)
        step(0, 0, False, True)
        with act.Fori(0, 3) as i:
            step(i * 2 + 1, 1, True, True)
            step(i * 2 + 2, 0, True, True)
        step(NB - 1, 1, True, False)
        x2_hi(NB - 1)

        act.wait_ge(routed, NB)
        nc.scalar.activation(disp[:], logit[:], ACT.Exp).then_inc(gexp_done, 1)
        for k in range(2):
            act.wait_ge(dt_ps, k + 1)
            act.copy(d_t[:, 4 * k:4 * k + 4, :].rearrange("q b n -> q (b n)"), ps[0:NT * E, 6 + k, 0:BK]
                     ).then_inc(dt_sb, 1)

        def chunk(c, first):
            for e in range(E):
                act.wait_ge(h_ready, c * E + e + 1)
                if not (first and e < 2):
                    act.wait_ge(prod_done, c * E + e - 1)
                nc.scalar.activation(sil[e % 2][:], ps[:, e % 2, 0:CH], ACT.Silu).then_inc(sil_done, 1)

        chunk(0, True)
        with act.Fori(1, NCH) as c:
            chunk(c, False)

    @block.tensor
    def _(pe):
        pe.wait_ge(pool_const, 11)
        for p in range(NPAIR):
            pe.wait_ge(x_loaded[p], 64)
            if p >= 1:
                pe.wait_ge(xt_sb, p)
            for t in range(NT):
                n = TW if t < NT - 1 else L - t * TW
                bank, o = divmod(t, 4)
                last = nc.tensor.transpose(ps[:, bank, o * TW:o * TW + n],
                                           xk[0:n, p, t, :, :].rearrange("q b c -> q (b c)"), ident[0:n, 0:n])
            last.then_inc(xt_ps, 1)
            if p == 0:
                pe.wait_ge(w_loaded, N_W_LOADS * 16)
            pe.wait_ge(xt_sb, p + 1)
            if p >= 1:
                pe.wait_ge(q_sb, p)
            for h in range(2):
                last = nc.tensor.matmul(ps[:, 2 + h, 0:HALF], wq_bd[:],
                                        x_t[:, p % 2, 4 + h * HALF:4 + (h + 1) * HALF], start=True, stop=True)
            last.then_inc(q_ps, 1)
            if p >= 1:
                pe.wait_ge(k_sb, p)
            for h in range(2):
                last = nc.tensor.matmul(ps[:, 4 + h, 0:L // 2], wk_bd[:],
                                        x_t[:, p % 2, h * (L // 2):(h + 1) * (L // 2)], start=True, stop=True)
            last.then_inc(k_ps, 1)
        pe.wait_ge(q_sb, NPAIR)
        pe.wait_ge(k_sb, NPAIR)

        def window_sums(p, half):
            pe.wait_ge(tanh_done, (p + 1) * 3)
            pe.wait_ge(h_sb, p + AHEAD)
            for r in range(3):
                for h in range(2):
                    for g in range(3):
                        src = th[:, half, :].rearrange("q (r n) -> q r n", n=QW)
                        last = nc.tensor.matmul(
                            ps[32 * g:32 * g + 32, h, 0:HALF], v_sel[:, r, :],
                            src[:, 3 * g + r, 8 + h * HALF:8 + (h + 1) * HALF], start=(r == 0), stop=(r == 2))
            last.then_inc(sc_ps, 1)
            pe.wait_ge(sc_sb, p + 1)
            pe.wait_ge(wt_copied, p + AHEAD)
            for t in range(NT):
                bank, o = divmod(t, 4)
                last = nc.tensor.transpose(ps[0:TW, 2 + bank, o * 96:o * 96 + 96], sc_s[:, t * TW:(t + 1) * TW],
                                           ident[0:96, 0:96])
            last.then_inc(sct_ps, 1)
            pe.wait_ge(band_ready, p + 1 + AHEAD)
            pe.wait_ge(bt_act, p * 2 + AHEAD)
            pe.wait_ge(bt_dve, p * 2 + AHEAD)
            for b in range(2):
                for k in range(2):
                    for t in range(4 * k, min(4 * k + 4, NT)):
                        o = t % 4
                        last = nc.tensor.transpose(ps[0:KW, 4 + 2 * b + k, o * TW:(o + 1) * TW],
                                                   band_a[:, b * NT + t, 0:KW], ident[0:TW, 0:TW])
                    last.then_inc(bt_ps, 1)
            pe.wait_ge(bt_act, (p + 1) * 2 + AHEAD)
            pe.wait_ge(bt_dve, (p + 1) * 2 + AHEAD)
            for b in range(2):
                for t in range(NT):
                    k = tile_n(t) + WIN - 1
                    last = nc.tensor.matmul(
                        ps[0:TW, b, t * C:(t + 1) * C], band_t[0:k, b * NT + t, :],
                        xk[0:k, bass.ds(p, 1), t, b, :].rearrange("q a c -> q (a c)"), start=True, stop=True)
            last.then_inc(h_ps, 1)

        with pe.Fori(0, NPAIR // 2) as i:
            for half in range(2):
                window_sums(i * 2 + half, half)

        def key_t(b, par):
            pe.wait_ge(xs_loaded, (b + 1) * 32)
            for t in range(NT):
                n = tile_n(t)
                bank, o = divmod(t, 4)
                last = nc.tensor.transpose(ps[:, 4 + bank, o * TW:o * TW + n],
                                           xs[par][0:n, t, :, :].rearrange("q k c -> q (k c)"), ident[0:n, 0:n])
            last.then_inc(kt_ps, 1)

        def query(b, par):
            pe.wait_ge(klo_sb, b + 1)
            for h in range(2):
                cols = slice(h * NQ, (h + 1) * NQ)
                nc.tensor.matmul(ps[:, 4 + h, 0:NQ], qw_r[:], k_hi[par][:, cols], start=True, stop=False)
                last = nc.tensor.matmul(ps[:, 4 + h, 0:NQ], qw_r[:], k_lo[par][:, cols], start=False, stop=True)
            last.then_inc(qq_ps, 1)

        def scores(b, par, j):
            n = (par + j) % 2
            m = tile_n(j)
            if j == 0:
                pe.wait_ge(qlo_sb, b + 1)
            for h in range(2):
                cols = slice(h * NQ, (h + 1) * NQ)
                for part in (k_hi, k_lo):
                    last = nc.tensor.matmul(ps[0:m, 2 * n + h, 0:NQ], part[par][:, j * TW:j * TW + m],
                                            q_s[par][:, cols], start=part is k_hi, stop=part is k_lo)
            last.then_inc(s_ps, 1)

        def values(b, par, j):
            n = (par + j) % 2
            m = tile_n(j)
            pe.wait_ge(sig_done, b * NT + j + 1)
            if j == 0:
                pe.wait_ge(o_sb, b)
            for h in range(2):
                last = nc.tensor.matmul(ps[h * C:(h + 1) * C, 6, 0:NQ], xs[par][0:m, j, 0, :], att[n][0:m, h, :],
                                        start=(j == 0), stop=(j == NT - 1))
            last.then_inc(av_done, 1)

        def back_waits(b):
            pe.wait_ge(o_sb, b + 1)
            pe.wait_ge(gate_sb, b + AHEAD)

        def back(b):
            for t in range(NT):
                last = nc.tensor.transpose(ps[0:TW, 7, t * C:(t + 1) * C], o_t[:, t * TW:(t + 1) * TW],
                                           ident[0:C, 0:C])
            last.then_inc(ot_ps, 1)

        def norm_t(b, nxt):
            pe.wait_ge(xn2_ready, b + 1)
            if nxt:
                pe.wait_ge(qlo_sb, b + 3)
            for t in range(NT):
                n = tile_n(t)
                bank, o = divmod(t, 4)
                last = nc.tensor.transpose(ps[:, 4 + bank, o * TW:o * TW + n],
                                           xn2[0:n, t, :, :].rearrange("q k c -> q (k c)"), ident[0:n, 0:n])
            last.then_inc(x2t_ps, 1)

        def gates(b):
            pe.wait_ge(x2_ready, b + 1)
            for t in range(NT):
                for part, w in enumerate((gw_hi, gw_lo)):
                    last = nc.tensor.matmul(ps[0:TW, 7, t * E:(t + 1) * E], x2_s[:, t * TW:(t + 1) * TW], w[:],
                                            start=(part == 0), stop=(part == 1))
            last.then_inc(gate_ps, 1)

        def step(b, par, tail, prep):
            scores(b, par, 0)
            scores(b, par, 1)
            if prep:
                key_t(b + 1, 1 - par)
            values(b, par, 0)
            if tail:
                back_waits(b - 1)
            scores(b, par, 2)
            if tail:
                back(b - 1)
            values(b, par, 1)
            scores(b, par, 3)
            values(b, par, 2)
            if prep:
                query(b + 1, 1 - par)
            scores(b, par, 4)
            values(b, par, 3)
            scores(b, par, 5)
            values(b, par, 4)
            if tail:
                norm_t(b - 1, prep)
            scores(b, par, 6)
            values(b, par, 5)
            values(b, par, 6)
            if tail:
                gates(b - 1)

        pe.wait_ge(h_sb, NPAIR + AHEAD)
        pe.wait_ge(act_const, 4)
        pe.wait_ge(dve_const, 4)
        key_t(0, 0)
        query(0, 0)
        step(0, 0, False, True)
        with pe.Fori(0, 3) as i:
            step(i * 2 + 1, 1, True, True)
            step(i * 2 + 2, 0, True, True)
        step(NB - 1, 1, True, False)
        back_waits(NB - 1)
        back(NB - 1)
        norm_t(NB - 1, False)
        gates(NB - 1)

        pe.wait_ge(disp_ready, 1)
        for k in range(2):
            for b in range(4):
                last = nc.tensor.transpose(ps[0:NT * E, 6 + k, b * TW:(b + 1) * TW],
                                           disp[:, 4 * k + b, :, :].rearrange("q t e -> q (t e)"),
                                           ident[0:TW, 0:TW])
            last.then_inc(dt_ps, 1)

        def expert(c, e, first):
            k = e % 2
            if not (first and e < 2):
                pe.wait_ge(prod_done, c * E + e - 1)
            xc = x3[:, bass.ds(c * CH, CH)]
            for j in range(2):
                nc.tensor.matmul(ps[:, 2 * j + k, 0:CH], w_hi[j][:, e, :], xc, start=True, stop=False)
                last = nc.tensor.matmul(ps[:, 2 * j + k, 0:CH], w_lo[j][:, e, :], xc, start=False, stop=True)
            last.then_inc(h_ready, 1)

        def project(c, p, first):
            pe.wait_ge(prod_done, c * E + 2 * p + 2)
            if not (first and p < 2):
                pe.wait_ge(scale_done, c * NPE + p - 1)
            for k in range(2):
                e = 2 * p + k
                last = nc.tensor.matmul(ps[k * C:(k + 1) * C, 4 + p % 2, 0:CH], w3_s[:, e, :], prod[e % 4][:],
                                        start=True, stop=True)
            last.then_inc(out_done, 1)

        def collect(c):
            pe.wait_ge(add_done, c * 7 + 7)
            pe.wait_ge(fin_done, c + AHEAD)
            for j in range(4):
                last = nc.tensor.matmul(ps[0:YT, 6, j * C:(j + 1) * C], acc_f[:, j * YT:(j + 1) * YT], stack2[:],
                                        start=True, stop=True)
            last.then_inc(y_done, 1)

        def chunk(c, first):
            for p in range(NPE):
                expert(c, 2 * p, first)
                expert(c, 2 * p + 1, first)
                if p > 0:
                    project(c, p - 1, first)
                elif not first:
                    project(c - 1, NPE - 1, False)
                if p == 2 and not first:
                    collect(c - 1)

        pe.wait_ge(x3_stored, NB * 16 + DMA_AHEAD)
        chunk(0, True)
        with pe.Fori(1, NCH) as c:
            chunk(c, False)
        project(NCH - 1, NPE - 1, False)
        collect(NCH - 1)

    @block.vector
    def _(dve):
        steps = [0]

        class Chain:

            def __init__(self, base):
                self.base, self.n = base, 0

            def link(self, ins):
                self.n += 1
                ins.then_inc(dve_step, 1)
                dve.wait_ge(dve_step, self.base + self.n)

        tt, ts = nc.vector.tensor_tensor, nc.vector.tensor_scalar

        nc.vector.memset(qb[:], 0.0).then_inc(dve_const, 1)
        nc.vector.memset(kx[:], 0.0)
        nc.vector.memset(sc_s[:, NW:NWP], 0.0)
        nc.vector.memset(v_sel[:], 0.0)
        for e in range(E):
            last = nc.vector.memset(rank[:, :, e:e + 1], float(E - e))
        last.then_inc(dve_const, 1)
        dve.wait_ge(dve_const, 2)
        dve.wait_ge(w_loaded, N_W_LOADS * 16)
        for k in range(2):
            for i in range(3):
                last = nc.vector.tensor_copy(v_sel[k * C:(k + 1) * C, i, 3 * k + i:3 * k + i + 1],
                                             v_col[k * C:(k + 1) * C, :])
        last.then_inc(dve_const, 1)
        for p in range(NPAIR):
            dve.wait_ge(k_ps, p + 1)
            nc.vector.tensor_copy(kx[:, p, 0:L].rearrange("q (h n) -> q h n", h=2), ps[:, 4:6, 0:L // 2]
                                  ).then_inc(k_sb, 1)

        def sums(p):
            for r in range(WIN):
                dst = th[:, bass.ds(p % 2, 1), :].rearrange("q a m -> q (a m)")[:, r * QW + r:r * QW + r + KXW]
                q = qb[:, bass.ds(p, 1), :].rearrange("q a n -> q (a n)")[:, r:r + KXW]
                k = kx[:, bass.ds(p, 1), :].rearrange("q a (s w) -> q (a s) w", w=WIN)[:, :, r:r + 1]
                last = tt(dst.rearrange("q (s w) -> q s w", w=WIN), q.rearrange("q (s w) -> q s w", w=WIN),
                          k.broadcast_to([128, SEG, WIN]), ALU.add)
                if r % 3 == 2:
                    last.then_inc(sum_done, 1)

        def softmax(p, chain):
            dve.wait_ge(sct_ps, p + 1)
            dve.wait_ge(band_ready, p + AHEAD)
            for b in range(2):
                for k in range(2):
                    n = 4 - k
                    src = ps[0:TW, 2 + k, 0:n * 96].rearrange("q (t g i) -> q t g i", t=n, g=3)
                    last = nc.vector.tensor_copy(
                        wt[:, b, 4 * k:4 * k + n, :].rearrange("q t (g i) -> q t g i", g=3),
                        src[:, :, :, 3 * b:3 * b + 3])
            last.then_inc(wt_copied, 1)
            dve.wait_ge(wt_copied, p + 1 + AHEAD)
            f = wt[:].rearrange("q b t r -> q (b t) r")
            chain.link(nc.vector.tensor_reduce(wt_max[:], f, AX.X, ALU.max))
            tt(f, f, wt_max[:].unsqueeze(2).broadcast_to([TW, 2 * NT, WIN]), ALU.subtract).then_inc(shifted, 1)
            dve.wait_ge(exp_done, p + 1)
            chain.link(nc.vector.tensor_reduce(wt_sum[:], f, AX.X, ALU.add))
            chain.link(nc.vector.reciprocal(wt_sum[:], wt_sum[:]))
            tt(f, f, wt_sum[:].unsqueeze(2).broadcast_to([TW, 2 * NT, WIN]), ALU.mult).then_inc(wt_ready, 1)

        def bands(p):
            for b in range(2):
                dve.wait_ge(bt_ps, p * 4 + 2 * b + 2 + AHEAD)
                nc.vector.tensor_copy(band_t[:, 7 * b + 4:7 * b + 7, :].rearrange("q t n -> q (t n)"),
                                      ps[0:KW, 5 + 2 * b, 0:3 * TW]).then_inc(bt_dve, 1)

        def norm_a(p, chain):
            dve.wait_ge(h_sb, p + 1 + AHEAD)
            h = h_all[:, bass.ds(p * 2, 2), :, :].rearrange("q b t c -> q (b t) c")
            chain.link(nc.vector.tensor_reduce(ln_s[:, 1, :], h, AX.X, ALU.add))
            ts(ln_s[:, 0, :], ln_s[:, 1, :], 1.0 / C, None, ALU.mult).then_inc(mean_ready, 1)
            dve.wait_ge(sq_ready, p + 1)
            chain.link(nc.vector.tensor_reduce(ln_s[:, 1, :], ln_sq[:], AX.X, ALU.add))
            ts(ln_s[:, 2, :], ln_s[:, 1, :], 1.0 / C, 1e-5, ALU.mult, ALU.add).then_inc(var_ready, 1)
            dve.wait_ge(rstd_ready, p + 1)
            tt(xn_all[:, bass.ds(p * 2, 2), :, :].rearrange("q b t c -> q (b t) c"), ln_c[:],
               ln_s[:, 3, :].unsqueeze(2).broadcast_to([TW, 2 * NT, C]), ALU.mult).then_inc(xn_ready, 1)

        A_LINKS = 5

        def pair(p, more):
            chain = Chain(p * A_LINKS)
            if more:
                dve.wait_ge(sc_ps, p + AHEAD)
                sums(p + 1)
            softmax(p, chain)
            bands(p)
            norm_a(p, chain)
            assert chain.n == A_LINKS

        dve.wait_ge(q_sb, NPAIR)
        dve.wait_ge(k_sb, NPAIR)
        sums(0)
        with dve.Fori(0, NPAIR - 1) as p:
            pair(p, True)
        pair(NPAIR - 1, False)
        dve.wait_ge(act_const, 4)
        tt(qw_r[C:128, :], qw_f[C:128, :], qw_r[C:128, :].bitcast(F32), ALU.subtract)
        tt(gw_lo[:], gw_f[:], gw_hi[:].bitcast(F32), ALU.subtract)
        for k in range(2):
            last = tt(w_lo[k][:].rearrange("d e h -> d (e h)"), w_f[k][:],
                      w_hi[k][:].rearrange("d e h -> d (e h)").bitcast(F32), ALU.subtract)
        last.then_inc(dve_const, 1)

        dve.wait_ge(xn_ready, NPAIR)
        for par in range(2):
            nc.vector.memset(k_hi[par][:, NW:NWP].bitcast(F32), 0.0)
            nc.vector.memset(k_lo[par][:, NW:NWP].bitcast(F32), 0.0)
        nc.vector.memset(x2_s[:, NW:NWP].bitcast(F32), 0.0)
        nc.vector.memset(x3[:, TOK:TOKP].bitcast(F32), 0.0)
        nc.vector.memset(zrow[:], 0.0)
        nc.vector.memset(o_t[:, NW:NWP], 0.0).then_inc(b_init, 1)

        def key_lo(b, par):
            dve.wait_ge(khi_sb, b + 1)
            tt(k_lo[par][:, 0:BK], ps[:, 4, 0:BK], k_hi[par][:, 0:BK].bitcast(F32), ALU.subtract)
            tt(k_lo[par][:, BK:NW], ps[:, 5, 0:NW - BK], k_hi[par][:, BK:NW].bitcast(F32), ALU.subtract
               ).then_inc(klo_sb, 1)

        def query_lo(b, par):
            dve.wait_ge(qhi_sb, b + 1)
            low = q_s[par][C:128, :].rearrange("q (h n) -> q h n", h=2)
            tt(low, ps[C:128, 4:6, 0:NQ], low.bitcast(F32), ALU.subtract).then_inc(qlo_sb, 1)

        def attended(b):
            dve.wait_ge(av_done, (b + 1) * NT)
            dve.wait_ge(ot_ps, b + AHEAD)
            nc.vector.tensor_copy(o_t[:, 0:NQ], ps[0:C, 6, 0:NQ])
            nc.vector.tensor_copy(o_t[:, NQ:NW], ps[C:128, 6, 0:NW - NQ]).then_inc(o_sb, 1)

        def residual(b, chain):
            dve.wait_ge(ot_ps, b + 1 + AHEAD)
            dve.wait_ge(h2_stored, b * 32 + DMA_AHEAD)
            tt(h2_s[:], ps[0:TW, 7, 0:NT * C].rearrange("q (t c) -> q t c", c=C),
               h_all[:, bass.ds(b, 1), :, :].rearrange("q a t c -> q (a t) c"), ALU.add).then_inc(h2_ready, 1)
            dve.wait_ge(h2_ready, b + 1)
            chain.link(nc.vector.tensor_reduce(bn_s[:, 1, :], h2_s[:], AX.X, ALU.add))
            ts(bn_s[:, 0, :], bn_s[:, 1, :], 1.0 / C, None, ALU.mult).then_inc(mean2, 1)

        def variance(b, chain):
            dve.wait_ge(sq2, b + 1)
            chain.link(nc.vector.tensor_reduce(bn_s[:, 1, :], bn_sq[:], AX.X, ALU.add))
            ts(bn_s[:, 2, :], bn_s[:, 1, :], 1.0 / C, 1e-5, ALU.mult, ALU.add).then_inc(var2, 1)

        def normed(b):
            dve.wait_ge(rstd2, b + 1)
            dve.wait_ge(x2t_ps, b + AHEAD)
            tt(xn2[:], bn_c[:].unsqueeze(2).broadcast_to([TW, NT, 2, C]),
               bn_s[:, 3, :].unsqueeze(2).unsqueeze(3).broadcast_to([TW, NT, 2, C]), ALU.mult).then_inc(xn2_ready, 1)

        def x2_lo(b):
            dve.wait_ge(x2hi_sb, b + 1)
            tt(x2_s[C:128, 0:BK], ps[C:128, 4, 0:BK], x2_s[C:128, 0:BK].bitcast(F32), ALU.subtract)
            tt(x2_s[C:128, BK:NW], ps[C:128, 5, 0:NW - BK], x2_s[C:128, BK:NW].bitcast(F32), ALU.subtract
               ).then_inc(x2_ready, 1)

        def route(b, chain):
            over = lambda v: v.unsqueeze(2).broadcast_to([TW, NT, E])
            lg = logit[:, bass.ds(b, 1), :, :].rearrange("q a t e -> q (a t) e")
            oh = onehot[:, bass.ds(b, 1), :, :].rearrange("q a t e -> q (a t) e")
            dve.wait_ge(gate_ps, b + 1)
            tt(r_a[:], ps[0:TW, 7, 0:NT * E].rearrange("q (t e) -> q t e", e=E),
               gb_row[:].unsqueeze(1).broadcast_to([TW, NT, E]), ALU.add).then_inc(gate_sb, 1)
            dve.wait_ge(gate_sb, b + 1 + AHEAD)
            chain.link(nc.vector.tensor_reduce(r_m[:, 0, :], r_a[:], AX.X, ALU.max))
            chain.link(tt(r_a[:], r_a[:], over(r_m[:, 0, :]), ALU.subtract))
            nc.vector.tensor_copy(lg, r_a[:])
            chain.link(nc.vector.scalar_tensor_tensor(r_b[:], r_a[:], 0.0, rank[:], ALU.is_equal, ALU.mult))
            chain.link(nc.vector.tensor_reduce(r_m[:, 1, :], r_b[:], AX.X, ALU.max))
            chain.link(tt(r_b[:], r_b[:], over(r_m[:, 1, :]), ALU.is_equal))
            chain.link(nc.vector.scalar_tensor_tensor(r_a[:], r_b[:], -BIG, r_a[:], ALU.mult, ALU.add))
            chain.link(nc.vector.tensor_reduce(r_m[:, 2, :], r_a[:], AX.X, ALU.max))
            chain.link(tt(r_a[:], r_a[:], over(r_m[:, 2, :]), ALU.is_equal))
            chain.link(tt(r_a[:], r_a[:], rank[:], ALU.mult))
            chain.link(nc.vector.tensor_reduce(r_m[:, 3, :], r_a[:], AX.X, ALU.max))
            chain.link(tt(r_c[:], r_a[:], over(r_m[:, 3, :]), ALU.is_equal))
            tt(oh, r_b[:], r_c[:], ALU.add).then_inc(routed, 1)

        B_LINKS = 13
        b_first = NPAIR * A_LINKS

        def step(b, par, tail, prep):
            chain = Chain((b - 1) * B_LINKS + b_first) if tail else None
            if tail:
                attended(b - 1)
            if prep:
                key_lo(b + 1, 1 - par)
            if tail:
                residual(b - 1, chain)
                variance(b - 1, chain)
                normed(b - 1)
            if prep:
                query_lo(b + 1, 1 - par)
            if tail:
                x2_lo(b - 1)
                route(b - 1, chain)
                assert chain.n == B_LINKS

        key_lo(0, 0)
        query_lo(0, 0)
        step(0, 0, False, True)
        with dve.Fori(0, 3) as i:
            step(i * 2 + 1, 1, True, True)
            step(i * 2 + 2, 0, True, True)
        step(NB - 1, 1, True, False)
        step(NB, 0, True, False)

        chain = Chain(b_first + NB * B_LINKS)
        dve.wait_ge(gexp_done, 1)
        d = disp[:].rearrange("q b t e -> q (b t) e")
        chain.link(tt(d, d, onehot[:].rearrange("q b t e -> q (b t) e"), ALU.mult))
        chain.link(nc.vector.tensor_reduce(d_sum[:, 0, :], d, AX.X, ALU.add))
        chain.link(nc.vector.reciprocal(d_sum[:, 1, :], d_sum[:, 0, :]))
        tt(d, d, d_sum[:, 1, :].unsqueeze(2).broadcast_to([TW, NB * NT, E]), ALU.mult).then_inc(disp_ready, 1)

        dve.wait_ge(h2_stored, NB * 32 + DMA_AHEAD)

        def product(c, e, first):
            dve.wait_ge(sil_done, c * E + e + 1)
            if not (first and e < 4):
                dve.wait_ge(out_done, c * NPE + e // 2 - 1)
            tt(prod[e % 4][:], sil[e % 2][:], ps[:, 2 + e % 2, 0:CH], ALU.mult).then_inc(prod_done, 1)

        def scale(c, p, first):
            dve.wait_ge(out_done, c * NPE + p + 1)
            dve.wait_ge(db_loaded[p % 4], (c * 2 + p // 4 + 1) * 32)
            if p >= 3:
                dve.wait_ge(add_done, c * 7 + p - 2)
            elif not first:
                dve.wait_ge(add_done, c * 7)
            dst = acc if p == 0 else res[p % 2]
            tt(dst[:], ps[:, 4 + p % 2, 0:CH], db[p % 4][:], ALU.mult).then_inc(scale_done, 1)

        def finish(c, first):
            dve.wait_ge(y_done, c + 1)
            dve.wait_ge(h2_loaded, (c + 1) * 16)
            if not first:
                dve.wait_ge(out_stored, c * 16 + DMA_AHEAD)
            tt(fin[:], ps[0:YT, 6, 0:4 * C].rearrange("q (j c) -> q j c", c=C), h2_c[:], ALU.add
               ).then_inc(fin_done, 1)

        def chunk(c, first):
            for p in range(NPE):
                product(c, 2 * p, first)
                product(c, 2 * p + 1, first)
                if p > 0:
                    scale(c, p - 1, first)
                elif not first:
                    scale(c - 1, NPE - 1, False)
                if p == 3 and not first:
                    finish(c - 1, False)

        chunk(0, True)
        with dve.Fori(1, NCH) as c:
            chunk(c, False)
        scale(NCH - 1, NPE - 1, False)
        finish(NCH - 1, False)

    ctx.close()


_INS = ["x", "L0_tok_W_qry", "L0_tok_W_key", "L0_tok_v", "L0_tok_b", "L0_attn_q_weight", "L0_ffn_gate_w",
        "L0_ffn_gate_b", "L0_ffn_w1", "L0_ffn_w2", "L0_ffn_w3"]


def kernel(**inputs):
    import numpy as _np
    import concourse.bacc as _bacc
    from concourse import mybir as _mybir
    from concourse.bass_utils import run_bass_kernel_spmd as _run

    nc = _bacc.Bacc("TRN2", target_bir_lowering=False, num_devices=1)
    arrays, args = {}, []
    for name in _INS:
        a = _np.ascontiguousarray(inputs[name])
        arrays[f"in_{name}"] = a
        args.append(nc.dram_tensor(f"in_{name}", a.shape, _mybir.dt.from_np(a.dtype), kind="ExternalInput").ap())
    out = nc.dram_tensor("out_0", (NB, NW, C), _mybir.dt.float32, kind="ExternalOutput").ap()
    build(nc, *args, out)
    r = _run(nc, [arrays], core_ids=[0])
    return r.results[0]["out_0"]
```

```python
from contextlib import ExitStack

import concourse.bass as bass
from concourse import mybir

F32 = mybir.dt.float32
F32R = mybir.dt.float32r
ALU = mybir.AluOpType
ACT = mybir.ActivationFunctionType
AX = mybir.AxisListType

NB, L, C = 8, 750, 64
WIN = 9
NW = L - WIN + 1
TW, NT = 108, 7
TL = NW - (NT - 1) * TW
KW = TW + WIN - 1
NPAIR = NB // 2
NWP = NT * TW
HALF = NW // 2
NQ = 372
BK = 4 * TW
SEG = 84
QW = 764
KXW = SEG * WIN
E, HID = 16, 128
TOK = NB * NW
CH, NCH = 496, 12
TOKP = CH * NCH
C_HALF = 4
YT = CH // 4
GB = NB // 2
NPE = E // 2
BIG = 3.0e38
AHEAD, DMA_AHEAD = 1, 16


def tile_n(t):
    return TW if t < NT - 1 else TL


def build(nc, x, wq_tok, wk_tok, v_tok, b_tok, q_weight, gate_w, gate_b, w1, w2, w3, out):
    ctx = ExitStack()
    place = [16512]

    def at(name, shape, dt=F32, offset=None):
        size = 4
        for n in shape[1:]:
            size *= n
        if offset is None:
            offset = place[0]
            place[0] += (size + 31) // 32 * 32
        return nc.alloc_sbuf_tensor_at(name, list(shape), dt, offset=offset)

    ident = at("ident", [128, 128])
    stack2 = at("stack2", [128, C])
    band = at("band", [TW, 13 * WIN])
    wq_bd = at("wq_bd", [128, 128])
    wk_bd = at("wk_bd", [128, 128])
    v_col = at("v_col", [128, 1])
    b_col = at("b_col", [128, 1])
    v_sel = at("v_sel", [128, 3, 32])
    qw_f = at("qw_f", [128, 128])
    qw_r = at("qw_r", [128, 128], F32R)
    gw_f = at("gw_f", [128, E])
    gw_r = at("gw_r", [128, 2, E], F32R)
    gb_row = at("gb_row", [TW, E])
    rank = at("rank", [TW, E])
    neg_half = at("neg_half", [TW, 2 * NT])
    w_f = [at(f"w{k}_f", [128, E * HID]) for k in (1, 2)]
    w_hi = [at(f"w{k}_hi", [128, E, HID], F32R) for k in (1, 2)]
    w_lo = [at(f"w{k}_lo", [128, E, HID], F32R) for k in (1, 2)]
    w3_s = at("w3_s", [HID, E, C])
    h_all = at("h_all", [TW, NB, NT, C])
    xn_all = at("xn_all", [TW, NB, NT, C])

    xk = at("xk", [KW, NPAIR, NT, 2, C])
    a_base = place[0]
    x_t = at("x_t", [128, 2, L])
    qb = at("qb", [128, NPAIR, QW])
    kx = at("kx", [128, NPAIR, KXW])
    sc_s = at("sc_s", [96, NWP])
    wt = at("wt", [TW, 2, NT, WIN])
    wt_max = at("wt_max", [TW, 2 * NT])
    wt_sum = at("wt_sum", [TW, 2 * NT])
    band_a = at("band_a", [TW, 2 * NT, 13 * WIN])
    band_t = at("band_t", [KW, 2 * NT, TW])
    ln_c = at("ln_c", [TW, 2 * NT, C])
    ln_sq = at("ln_sq", [TW, 2 * NT, C])
    ln_s = at("ln_s", [TW, 4, 2 * NT])
    a_end = place[0]
    t_base = place[0]
    th = at("th", [128, 2, WIN * QW])
    t_end = place[0]

    place[0] = a_base
    xs = [at(f"xs{p}", [TW, NT, 2, C]) for p in range(2)]
    k_hi = [at(f"k_hi{p}", [128, NWP], F32R) for p in range(2)]
    k_lo = [at(f"k_lo{p}", [128, NWP], F32R) for p in range(2)]
    q_s = [at(f"q_s{p}", [128, 2 * NQ], F32R) for p in range(2)]
    att = [at(f"att{p}", [TW, 2, NQ]) for p in range(2)]
    tail_base = place[0]
    o_t = at("o_t", [C, NWP])
    assert place[0] <= t_base
    bn_c = at("bn_c", [TW, NT, C])
    assert place[0] <= a_end
    place[0] = t_base
    x3 = at("x3", [128, TOKP], F32R)
    c_base = place[0]
    h2_s = at("h2_s", [TW, NT, C])
    xn2 = at("xn2", [TW, NT, 2, C])
    x2_s = at("x2_s", [128, NWP], F32R)
    bn_sq = at("bn_sq", [TW, NT, C])
    bn_s = at("bn_s", [TW, 4, NT])
    r_a = at("r_a", [TW, GB * NT, E])
    r_b = at("r_b", [TW, GB * NT, E])
    r_m = at("r_m", [TW, 4, GB * NT])
    logit = at("logit", [TW, NB, NT, E])
    r_w = at("r_w", [TW, 2, GB * NT])
    zrow = at("zrow", [E, C])
    d_t = at("d_t", [NT * E, NB, TW])
    assert place[0] <= t_end
    place[0] = a_base
    sil = [at(f"sil{k}", [HID, CH]) for k in range(2)]
    prod = [at(f"prod{k}", [HID, CH]) for k in range(4)]
    db = [at(f"db{k}", [128, CH]) for k in range(4)]
    res = [at(f"res{k}", [128, CH]) for k in range(2)]
    acc = at("acc", [128, CH])
    acc_f = at("acc_f", [128, CH])
    h2_c = at("h2_c", [YT, 4, C])
    fin = at("fin", [YT, 4, C])
    assert place[0] <= tail_base

    h2_d = nc.dram_tensor("h2_d", [TOKP, C], F32).ap()
    dt_d = nc.dram_tensor("dt_d", [E, TOKP], F32).ap()

    ps = ctx.enter_context(nc.psum_tensor("ps", [128, 8, 512], F32))

    def sem(name):
        return ctx.enter_context(nc.semaphore(name))

    tok_loaded, w_loaded, pool_const, dve_const, act_const = (
        sem(n) for n in ("tok_loaded", "w_loaded", "pool_const", "dve_const", "act_const"))
    sums_read = sem("sums_read")
    w_split = sem("w_split")
    x_loaded = [sem(f"x_loaded{p}") for p in range(NPAIR)]
    xt_ps, xt_sb, q_ps, q_sb, k_ps, k_sb = (sem(n) for n in ("xt_ps", "xt_sb", "q_ps", "q_sb", "k_ps", "k_sb"))
    sum_done, tanh_done, sc_ps, sc_sb, sct_ps, wt_copied = (
        sem(n) for n in ("sum_done", "tanh_done", "sc_ps", "sc_sb", "sct_ps", "wt_copied"))
    shifted, exp_done, wt_ready, band_ready, bt_ps = (
        sem(n) for n in ("shifted", "exp_done", "wt_ready", "band_ready", "bt_ps"))
    bt_sb, h_ps, h_sb = (sem(n) for n in ("bt_sb", "h_ps", "h_sb"))
    mean_ready, sq_ready, var_ready, rstd_ready, xn_ready = (
        sem(n) for n in ("mean_ready", "sq_ready", "var_ready", "rstd_ready", "xn_ready"))
    xs_loaded, kt_ps, khi_sb, klo_sb, qq_ps, qhi_sb, qlo_sb = (
        sem(n) for n in ("xs_loaded", "kt_ps", "khi_sb", "klo_sb", "qq_ps", "qhi_sb", "qlo_sb"))
    s_ps, sig_done, av_done, o_sb, ot_ps, h2_ready, h2_stored = (
        sem(n) for n in ("s_ps", "sig_done", "av_done", "o_sb", "ot_ps", "h2_ready", "h2_stored"))
    mean2, sq2, var2, rstd2, xn2_ready, x2t_ps, x2hi_sb, x2_ready, x3_stored = (
        sem(n) for n in ("mean2", "sq2", "var2", "rstd2", "xn2_ready", "x2t_ps", "x2hi_sb", "x2_ready", "x3_stored"))
    gate_ps, gate_sb, b_init, routed, rw_ready, disp_ready, dt_ps, dt_sb, dt_stored = (
        sem(n) for n in ("gate_ps", "gate_sb", "b_init", "routed", "rw_ready", "disp_ready", "dt_ps", "dt_sb",
                         "dt_stored"))
    pad_stored = sem("pad_stored")
    h_ready, sil_done, prod_done, out_done, scale_done, add_done, y_done, fin_done = (
        sem(n) for n in ("h_ready", "sil_done", "prod_done", "out_done", "scale_done", "add_done", "y_done",
                         "fin_done"))
    db_loaded = [sem(f"db_loaded{k}") for k in range(4)]
    h2_loaded, out_stored = sem("h2_loaded"), sem("out_stored")
    dve_step, pool_step = sem("dve_step"), sem("pool_step")

    out_rows = out.rearrange("b n c -> (b n) c")
    N_TOK_LOADS, N_W_LOADS = 2 * 2 + 2, 2 * 5 + 2

    block = ctx.enter_context(nc.Block())

    @block.sync
    def _(sp):
        for p in range(NPAIR):
            for b in range(2):
                xb = x[2 * p + b]
                rows = bass.AP(xb.tensor, xb.offset, [[C, KW], [TW * C, NT - 1], [1, C]])
                sp.dma_start(xk[:, p, 0:NT - 1, b, :], rows).then_inc(x_loaded[p], 16)
                sp.dma_start(xk[0:TL + WIN - 1, p, NT - 1, b, :], xb[(NT - 1) * TW:L, :]).then_inc(x_loaded[p], 16)

        halves = (slice(0, C), slice(C, 128))

        def load(dst, src):
            sp.dma_start(dst, src).then_inc(w_loaded, 16)

        for half in halves:
            load(qw_f[half, 0:C], q_weight)
            load(qw_f[half, C:128], q_weight)
            load(gw_f[half, :], gate_w)
            for w, dst in ((w1, w_f[0]), (w2, w_f[1])):
                load(dst[half, :].rearrange("d (e h) -> d e h", h=HID), w.rearrange("e d h -> d e h"))
        load(gb_row[:], gate_b.rearrange("(a e) -> a e", a=1).broadcast_to([TW, E]))
        load(w3_s[:], w3.rearrange("e h o -> h e o"))

        def stage_in(b, par):
            sp.wait_ge(xs_loaded, b * 32)
            for k in range(2):
                sp.dma_start(xs[par][:, :, k, :], xn_all[:, bass.ds(b, 1), :, :].rearrange("p a t c -> p (a t) c")
                             ).then_inc(xs_loaded, 16)

        def store_h2(b):
            sp.wait_ge(h2_ready, b + 1)
            rows = h2_d[bass.ds(b * NW, (NT - 1) * TW), :].rearrange("(t p) c -> p t c", p=TW)
            sp.dma_start(rows, h2_s[:, 0:NT - 1, :]).then_inc(h2_stored, 16)
            sp.dma_start(h2_d[bass.ds(b * NW + (NT - 1) * TW, TL), :], h2_s[0:TL, NT - 1, :]).then_inc(h2_stored, 16)

        def store_x3(b):
            sp.wait_ge(x2_ready, b + 1)
            sp.dma_start(x3[:, bass.ds(b * NW, NW)].bitcast(F32), x2_s[:, 0:NW].bitcast(F32)).then_inc(x3_stored, 16)

        def step(b, par, more, tail, lag):
            if lag:
                store_x3(b - 2)
            if tail:
                store_h2(b - 1)
            if more:
                sp.wait_ge(av_done, (b + 1) * NT)
                stage_in(b + 2, par)

        sp.wait_ge(sums_read, 1)
        sp.wait_ge(xn_ready, 1)
        sp.wait_ge(xt_sb, NPAIR)
        sp.wait_ge(k_ps, NPAIR)
        stage_in(0, 0)
        stage_in(1, 1)
        sp.wait_ge(xn_ready, NPAIR)
        sp.wait_ge(b_init, 1)
        sp.dma_start(h2_d[TOK:TOKP, :], zrow[0:TOKP - TOK, :]).then_inc(pad_stored, 16)
        sp.dma_start(dt_d[:, TOK:TOKP], zrow[:, 0:TOKP - TOK]).then_inc(pad_stored, 16)
        step(0, 0, True, False, False)
        step(1, 1, True, True, False)
        with sp.Fori(0, 2) as i:
            step(i * 2 + 2, 0, True, True, True)
            step(i * 2 + 3, 1, True, True, True)
        step(6, 0, False, True, True)
        step(7, 1, False, True, True)

        def store_dt(g):
            sp.wait_ge(dt_sb, g + 1)
            for b in range(g * GB, (g + 1) * GB):
                rows = bass.AP(dt_d.tensor, dt_d.offset + b * NW, [[TW, NT - 1], [TOKP, E], [1, TW]])
                sp.dma_start(rows, d_t[0:(NT - 1) * E, b, :]).then_inc(dt_stored, 16)
                sp.dma_start(dt_d[:, b * NW + (NT - 1) * TW:(b + 1) * NW],
                             d_t[(NT - 1) * E:NT * E, b, 0:TL]).then_inc(dt_stored, 16)

        def load_db(c, p):
            src = dt_d[2 * p:2 * p + 2, bass.ds(c * CH, CH)].unsqueeze(1).broadcast_to([2, C, CH])
            sp.dma_start(db[p % 4][:], src).then_inc(db_loaded[p % 4], 16)

        def load_h2(c):
            rows = h2_d[bass.ds(c * CH, CH), :].rearrange("(j p) c -> p j c", p=YT)
            sp.dma_start(h2_c[:, :, :], rows).then_inc(h2_loaded, 16)

        def chunk(c, late=False):
            for p in range(NPE):
                sp.wait_ge(scale_done, c * NPE + p - 3)
                load_db(c, p)
                if late and p == 4:
                    store_dt(1)
                if p == 6:
                    sp.wait_ge(fin_done, c + AHEAD)
                    sp.dma_start(out_rows[bass.ds((c - 1) * CH, CH), :].rearrange("(j p) c -> p j c", p=YT),
                                 fin[:, :, :]).then_inc(out_stored, 16)
                    load_h2(c)

        store_dt(0)
        sp.wait_ge(dt_stored, GB * 2 * 16)
        sp.wait_ge(h2_stored, (NB - 1) * 32 + DMA_AHEAD)
        for p in range(4):
            load_db(0, p)
        store_x3(NB - 2)
        load_h2(0)
        for p in range(4, NPE):
            sp.wait_ge(scale_done, p - 3)
            if p == NPE - 1:
                store_h2(NB - 1)
            load_db(0, p)
        with sp.Fori(1, 2) as c:
            chunk(c)
        store_x3(NB - 1)
        with sp.Fori(2, 3) as c:
            chunk(c, late=True)
        with sp.Fori(3, C_HALF) as c:
            chunk(c)
        sp.wait_ge(dt_stored, NB * 2 * 16)
        sp.wait_ge(pad_stored, 32)
        sp.wait_ge(h2_stored, NB * 32 + DMA_AHEAD)
        with sp.Fori(C_HALF, NCH) as c:
            chunk(c)
        sp.wait_ge(fin_done, NCH + AHEAD)
        base = (NCH - 1) * CH
        sp.dma_start(out_rows[base:base + 3 * YT, :].rearrange("(j p) c -> p j c", p=YT),
                     fin[:, 0:3, :]).then_inc(out_stored, 16)
        sp.dma_start(out_rows[base + 3 * YT:TOK, :], fin[0:TOK - base - 3 * YT, 3, :]).then_inc(out_stored, 16)
        sp.wait_ge(out_stored, (NCH + 1) * 16 + DMA_AHEAD)

    @block.gpsimd
    def _(pool):
        for s in (ot_ps, x2t_ps, gate_sb,
                  gate_ps, fin_done):
            pool.sem_inc(s, AHEAD)
        for s in (h2_stored, x3_stored, out_stored):
            pool.sem_inc(s, DMA_AHEAD)
        nc.gpsimd.memset(wq_bd[:], 0.0).then_inc(pool_const, 1)
        nc.gpsimd.memset(wk_bd[:], 0.0).then_inc(pool_const, 1)
        nc.gpsimd.memset(ident[:], 0.0).then_inc(pool_const, 1)
        nc.gpsimd.memset(stack2[:], 0.0).then_inc(pool_const, 1)
        nc.gpsimd.memset(band[:], 1.0).then_inc(pool_const, 1)
        nc.gpsimd.memset(neg_half[:], -0.5).then_inc(pool_const, 1)
        pool.wait_ge(pool_const, 6)
        nc.gpsimd.affine_select(out=ident[:], in_=ident[:], compare_op=ALU.not_equal, fill=1.0, base=0,
                                pattern=[[-1, 128]], channel_multiplier=1).then_inc(pool_const, 1)
        nc.gpsimd.affine_select(out=stack2[:], in_=stack2[:], compare_op=ALU.not_equal, fill=1.0, base=0,
                                pattern=[[-1, C]], channel_multiplier=1).then_inc(pool_const, 1)
        nc.gpsimd.affine_select(out=band[:], in_=band[:], compare_op=ALU.is_ge, fill=0.0, base=0,
                                pattern=[[1, 13 * WIN]], channel_multiplier=-1).then_inc(pool_const, 1)
        pool.wait_ge(pool_const, 9)
        nc.gpsimd.affine_select(out=stack2[:], in_=stack2[:], compare_op=ALU.not_equal, fill=1.0, base=-C,
                                pattern=[[-1, C]], channel_multiplier=1).then_inc(pool_const, 1)
        nc.gpsimd.affine_select(out=band[:], in_=band[:], compare_op=ALU.is_ge, fill=0.0, base=WIN - 1,
                                pattern=[[-1, 13 * WIN]], channel_multiplier=1).then_inc(pool_const, 1)

        def norm_a(p):
            h = h_all[:, bass.ds(p * 2, 2), :, :].rearrange("q b t c -> q (b t) c")
            pool.wait_ge(mean_ready, p + 1)
            nc.gpsimd.tensor_tensor(ln_c[:], h, ln_s[:, 0, :].unsqueeze(2).broadcast_to([TW, 2 * NT, C]),
                                    ALU.subtract).then_inc(pool_step, 1)
            pool.wait_ge(pool_step, p + 1)
            nc.gpsimd.tensor_tensor(ln_sq[:], ln_c[:], ln_c[:], ALU.mult).then_inc(sq_ready, 1)

        def bands(p):
            pool.wait_ge(wt_ready, p + 1)
            if p:
                pool.wait_ge(bt_ps, p * 4)
            m = band[:].rearrange("q (u r) -> q u r", r=WIN).unsqueeze(1).broadcast_to([TW, NT, 13, WIN])
            for b in range(2):
                f = wt[:, b, :, :].unsqueeze(2).broadcast_to([TW, NT, 13, WIN])
                nc.gpsimd.tensor_tensor(band_a[:, b * NT:(b + 1) * NT, :].rearrange("q n (u r) -> q n u r", r=WIN),
                                        f, m, ALU.mult).then_inc(band_ready, 1)

        def rstd_a(p):
            pool.wait_ge(var_ready, p + 1)
            nc.gpsimd.tensor_tensor(ln_s[:, 3, :], ln_s[:, 2, :], neg_half[:], ALU.pow).then_inc(rstd_ready, 1)

        for p in range(NPAIR):
            bands(p)
            if p > 1:
                rstd_a(p - 2)
            if p > 0:
                norm_a(p - 1)
        rstd_a(NPAIR - 2)
        norm_a(NPAIR - 1)
        rstd_a(NPAIR - 1)

        def centre(b):
            pool.wait_ge(mean2, b + 1)
            nc.gpsimd.tensor_tensor(bn_c[:], h2_s[:], bn_s[:, 0, :].unsqueeze(2).broadcast_to([TW, NT, C]),
                                    ALU.subtract).then_inc(pool_step, 1)
            pool.wait_ge(pool_step, b + NPAIR + 1)
            nc.gpsimd.tensor_tensor(bn_sq[:], bn_c[:], bn_c[:], ALU.mult).then_inc(sq2, 1)

        def normed(b):
            pool.wait_ge(var2, b + 1)
            nc.gpsimd.tensor_tensor(bn_s[:, 3, :], bn_s[:, 2, :], neg_half[:, 0:NT], ALU.pow).then_inc(rstd2, 1)
            pool.wait_ge(rstd2, b + 1)
            pool.wait_ge(x2t_ps, b + AHEAD)
            nc.gpsimd.tensor_tensor(xn2[:], bn_c[:].unsqueeze(2).broadcast_to([TW, NT, 2, C]),
                                    bn_s[:, 3, :].unsqueeze(2).unsqueeze(3).broadcast_to([TW, NT, 2, C]),
                                    ALU.mult).then_inc(xn2_ready, 1)

        with pool.Fori(0, NB - 1) as b:
            centre(b)
            normed(b)

        def chunk(c, first):
            for p in range(1, NPE):
                pool.wait_ge(scale_done, c * NPE + p + 1)
                pool.wait_ge(add_done, c * 7 + p - 1)
                if p < NPE - 1:
                    nc.gpsimd.tensor_tensor(acc[:], acc[:], res[p % 2][:], ALU.add).then_inc(add_done, 1)
                else:
                    if not first:
                        pool.wait_ge(y_done, c)
                    nc.gpsimd.tensor_tensor(acc_f[:], acc[:], res[p % 2][:], ALU.add).then_inc(add_done, 1)
                if first and p == 2:
                    centre(NB - 1)
                if first and p == 4:
                    normed(NB - 1)

        chunk(0, True)
        with pool.Fori(1, NCH) as c:
            chunk(c, False)

    @block.scalar
    def _(act):
        def twice(v):
            return v.rearrange("(a p b) -> a p b", a=1, b=1).broadcast_to([2, C, 1])

        halves = (slice(0, C), slice(C, 128))
        act.dma_start(b_col[:], twice(b_tok)).then_inc(tok_loaded, 16)
        act.dma_start(v_col[:], twice(v_tok)).then_inc(tok_loaded, 16)
        act.wait_ge(pool_const, 2)
        for half in halves:
            act.dma_start(wq_bd[half, half], wq_tok).then_inc(tok_loaded, 16)
            act.dma_start(wk_bd[half, half], wk_tok).then_inc(tok_loaded, 16)

        def tokens_out(p):
            act.wait_ge(xt_ps, p + 1)
            if p >= 2:
                act.wait_ge(k_ps, p - 1)
            bank = 6 * (p % 2)
            act.copy(x_t[:, p % 2, 0:BK], ps[:, bank, 0:BK])
            act.copy(x_t[:, p % 2, BK:L], ps[:, bank + 1, 0:L - BK]).then_inc(xt_sb, 1)

        def projected(p):
            act.wait_ge(q_ps, p + 1)
            if p == 0:
                act.wait_ge(tok_loaded, N_TOK_LOADS * 16)
            nc.scalar.activation(qb[:, p, 8:8 + NW].rearrange("q (h n) -> q h n", h=2), ps[:, 2:4, 0:HALF],
                                 ACT.Identity, bias=b_col[:]).then_inc(q_sb, 1)
            act.wait_ge(k_ps, p + 1)
            act.copy(kx[:, p, 0:L].rearrange("q (h n) -> q h n", h=2), ps[:, 4:6, 0:L // 2]).then_inc(k_sb, 1)

        def exps(p):
            act.wait_ge(shifted, p + 1)
            nc.scalar.activation(wt[:], wt[:], ACT.Exp).then_inc(exp_done, 1)

        def tanhs(p, i):
            act.wait_ge(sum_done, p * 3 + i + 1)
            v = th[:, p % 2, :].rearrange("q (r n) -> q r n", n=QW)[:, 3 * i:3 * i + 3, 8:8 + NW]
            nc.scalar.activation(v, v, ACT.Tanh).then_inc(tanh_done, 1)

        def scores_out(p):
            act.wait_ge(sc_ps, p + 1)
            if p:
                act.wait_ge(sct_ps, p)
            act.copy(sc_s[:, 0:NW].rearrange("q (h n) -> q h n", h=2), ps[0:96, 0:2, 0:HALF]).then_inc(sc_sb, 1)

        def bands_out(p):
            for b in range(2):
                for k in range(2):
                    n = 4 - k
                    act.wait_ge(bt_ps, p * 4 + 2 * b + k + 1)
                    last = act.copy(band_t[:, 7 * b + 4 * k:7 * b + 4 * k + n, :].rearrange("q t n -> q (t n)"),
                                    ps[0:KW, 4 + 2 * b + k, 0:n * TW])
            last.then_inc(bt_sb, 1)

        def sums_out(p):
            act.wait_ge(h_ps, p + 1)
            act.copy(h_all[:, 2 * p:2 * p + 2, :, :].rearrange("q b t c -> q b (t c)"),
                     ps[0:TW, 4:6, 0:NT * C]).then_inc(h_sb, 1)

        tokens_out(0)
        tokens_out(1)
        projected(0)
        tokens_out(2)
        projected(1)
        tanhs(0, 0)
        tokens_out(3)
        projected(2)
        tanhs(0, 1)
        projected(3)
        tanhs(0, 2)
        for p in range(NPAIR):
            more = p + 1 < NPAIR
            if p > 0:
                exps(p - 1)
            if more:
                tanhs(p + 1, 0)
            if p > 1:
                sums_out(p - 2)
            if more:
                tanhs(p + 1, 1)
            scores_out(p)
            if p > 0:
                bands_out(p - 1)
            if more:
                tanhs(p + 1, 2)
            if p == 1:
                act.wait_ge(w_loaded, N_W_LOADS * 16)
                act.copy(qw_r[:], qw_f[:]).then_inc(act_const, 1)
                act.copy(gw_r[:, 0, :], gw_f[:]).then_inc(act_const, 1)
                for k in range(2):
                    act.copy(w_hi[k][:].rearrange("d e h -> d (e h)"), w_f[k][:]).then_inc(act_const, 1)
        exps(NPAIR - 1)
        sums_out(NPAIR - 2)

        def key_hi(b, par, bank=4):
            act.wait_ge(kt_ps, b + 1)
            act.copy(k_hi[par][:, 0:BK], ps[:, bank, 0:BK])
            act.copy(k_hi[par][:, BK:NW], ps[:, bank + 1, 0:NW - BK]).then_inc(khi_sb, 1)

        def query_hi(b, par, bank=4):
            act.wait_ge(qq_ps, b + 1)
            act.copy(q_s[par][:].rearrange("q (h n) -> q h n", h=2), ps[:, bank:bank + 2, 0:NQ]).then_inc(qhi_sb, 1)

        def sigmoid(b, par, j, tail):
            n = (par + j) % 2
            act.wait_ge(s_ps, b * NT + j + 1)
            if j >= 2 or tail:
                act.wait_ge(av_done, b * NT + j - 1)
            nc.scalar.activation(att[n][0:tile_n(j)], ps[0:tile_n(j), 2 * n:2 * n + 2, 0:NQ],
                                 ACT.Sigmoid).then_inc(sig_done, 1)

        def x2_hi(b, bank=4):
            act.wait_ge(x2t_ps, b + 1 + AHEAD)
            act.wait_ge(x3_stored, b * 16 + DMA_AHEAD)
            act.wait_ge(gate_ps, b + AHEAD)
            act.copy(x2_s[:, 0:BK], ps[:, bank, 0:BK])
            act.copy(x2_s[:, BK:NW], ps[:, bank + 1, 0:NW - BK]).then_inc(x2hi_sb, 1)

        def dispatch_weights(g):
            act.wait_ge(routed, g + 1)
            nc.scalar.activation(r_w[:, 0, :], r_m[:, 2, :], ACT.Sigmoid, scale=-1.0)
            nc.scalar.activation(r_w[:, 1, :], r_m[:, 2, :], ACT.Sigmoid).then_inc(rw_ready, 1)

        def dispatch_out(g, bank):
            act.wait_ge(dt_ps, g + 1)
            act.copy(d_t[:, g * GB:(g + 1) * GB, :].rearrange("q b n -> q (b n)"), ps[0:NT * E, bank, 0:BK]
                     ).then_inc(dt_sb, 1)

        def step(b, par, prep, tail, lag):
            sigmoid(b, par, 0, tail)
            sigmoid(b, par, 1, tail)
            if lag:
                x2_hi(b - 2)
            sigmoid(b, par, 2, tail)
            sigmoid(b, par, 3, tail)
            if prep:
                key_hi(b + 1, 1 - par)
            else:
                dispatch_weights(0)
            sigmoid(b, par, 4, tail)
            sigmoid(b, par, 5, tail)
            if prep:
                query_hi(b + 1, 1 - par)
            sigmoid(b, par, 6, tail)
            if not prep:
                dispatch_out(0, 4)

        act.wait_ge(sums_read, 1)
        key_hi(0, 0, 0)
        bands_out(NPAIR - 1)
        query_hi(0, 0, 0)
        sums_out(NPAIR - 1)
        step(0, 0, True, False, False)
        step(1, 1, True, True, False)
        with act.Fori(0, 2) as i:
            step(i * 2 + 2, 0, True, True, True)
            step(i * 2 + 3, 1, True, True, True)
        step(6, 0, True, True, True)
        step(7, 1, False, True, True)

        def silu(c, e, first):
            act.wait_ge(h_ready, c * E + e + 1)
            if not (first and e < 2):
                act.wait_ge(prod_done, c * E + e - 1)
            nc.scalar.activation(sil[e % 2][:], ps[:, e % 2, 0:CH], ACT.Silu).then_inc(sil_done, 1)

        for e in range(E):
            silu(0, e, True)
            if e == 1:
                x2_hi(NB - 2, 6)
        x2_hi(NB - 1, 6)
        with act.Fori(1, 2) as c:
            for e in range(E):
                silu(c, e, False)
                if e == 13:
                    dispatch_weights(1)
        with act.Fori(2, 3) as c:
            for e in range(E):
                silu(c, e, False)
                if e == 3:
                    dispatch_out(1, 7)
        with act.Fori(3, NCH) as c:
            for e in range(E):
                silu(c, e, False)

    @block.tensor
    def _(pe):
        pe.wait_ge(pool_const, 11)
        def tokens_t(p):
            pe.wait_ge(x_loaded[p], 64)
            if p >= 2:
                pe.wait_ge(xt_sb, p - 1)
            for t in range(NT):
                n = TW if t < NT - 1 else L - t * TW
                bank, o = divmod(t, 4)
                last = nc.tensor.transpose(ps[:, 6 * (p % 2) + bank, o * TW:o * TW + n],
                                           xk[0:n, p, t, :, :].rearrange("q b c -> q (b c)"), ident[0:n, 0:n])
            last.then_inc(xt_ps, 1)

        def project_in(p):
            if p == 0:
                pe.wait_ge(tok_loaded, N_TOK_LOADS * 16)
            pe.wait_ge(xt_sb, p + 1)
            if p >= 1:
                pe.wait_ge(q_sb, p)
            for h in range(2):
                last = nc.tensor.matmul(ps[:, 2 + h, 0:HALF], wq_bd[:],
                                        x_t[:, p % 2, 4 + h * HALF:4 + (h + 1) * HALF], start=True, stop=True)
            last.then_inc(q_ps, 1)
            if p >= 1:
                pe.wait_ge(k_sb, p)
            for h in range(2):
                last = nc.tensor.matmul(ps[:, 4 + h, 0:L // 2], wk_bd[:],
                                        x_t[:, p % 2, h * (L // 2):(h + 1) * (L // 2)], start=True, stop=True)
            last.then_inc(k_ps, 1)

        tokens_t(0)
        for p in range(NPAIR):
            if p + 1 < NPAIR:
                tokens_t(p + 1)
            project_in(p)
        pe.wait_ge(q_sb, NPAIR)
        pe.wait_ge(k_sb, NPAIR)

        def token_scores(p, i):
            pe.wait_ge(tanh_done, p * 3 + i + 1)
            if i == 0 and p:
                pe.wait_ge(sc_sb, p)
            src = th[:, p % 2, :].rearrange("q (r n) -> q r n", n=QW)
            for h in range(2):
                for g in range(3):
                    last = nc.tensor.matmul(
                        ps[32 * g:32 * g + 32, h, 0:HALF], v_sel[:, i, :],
                        src[:, 3 * i + g, 8 + h * HALF:8 + (h + 1) * HALF], start=(i == 0), stop=(i == 2))
            if i == 2:
                last.then_inc(sc_ps, 1)

        def scores_t(p):
            pe.wait_ge(sc_sb, p + 1)
            if p:
                pe.wait_ge(wt_copied, p)
            for t in range(NT):
                bank, o = divmod(t, 4)
                last = nc.tensor.transpose(ps[0:TW, 2 + bank, o * 96:o * 96 + 96], sc_s[:, t * TW:(t + 1) * TW],
                                           ident[0:96, 0:96])
            last.then_inc(sct_ps, 1)

        def bands_t(p):
            if p:
                pe.wait_ge(h_sb, p)
            for b in range(2):
                pe.wait_ge(band_ready, 2 * p + b + 1)
                for k in range(2):
                    for t in range(4 * k, min(4 * k + 4, NT)):
                        o = t % 4
                        last = nc.tensor.transpose(ps[0:KW, 4 + 2 * b + k, o * TW:(o + 1) * TW],
                                                   band_a[:, b * NT + t, 0:KW], ident[0:TW, 0:TW])
                    last.then_inc(bt_ps, 1)

        def window_sums(p):
            pe.wait_ge(bt_sb, p + 1)
            for b in range(2):
                for t in range(NT):
                    k = tile_n(t) + WIN - 1
                    last = nc.tensor.matmul(ps[0:TW, 4 + b, t * C:(t + 1) * C], band_t[0:k, b * NT + t, :],
                                            xk[0:k, p, t, b, :], start=True, stop=True)
            last.then_inc(h_ps, 1)

        pe.wait_ge(dve_const, 3)
        for p in range(NPAIR):
            token_scores(p, 0)
            if p > 0:
                scores_t(p - 1)
            token_scores(p, 1)
            if p > 1:
                window_sums(p - 2)
            token_scores(p, 2)
            if p > 0:
                bands_t(p - 1)
        scores_t(NPAIR - 1)
        window_sums(NPAIR - 2)

        def key_t(b, par, lag=False, first=4):
            if lag:
                pe.wait_ge(x2_ready, b - 2)
            pe.wait_ge(xs_loaded, (b + 1) * 32)
            for t in range(NT):
                n = tile_n(t)
                bank, o = divmod(t, 4)
                last = nc.tensor.transpose(ps[:, first + bank, o * TW:o * TW + n],
                                           xs[par][0:n, t, :, :].rearrange("q k c -> q (k c)"), ident[0:n, 0:n])
            last.then_inc(kt_ps, 1)

        def query(b, par, first=4):
            pe.wait_ge(klo_sb, b + 1)
            for h in range(2):
                cols = slice(h * NQ, (h + 1) * NQ)
                nc.tensor.matmul(ps[:, first + h, 0:NQ], qw_r[:], k_hi[par][:, cols], start=True, stop=False)
                last = nc.tensor.matmul(ps[:, first + h, 0:NQ], qw_r[:], k_lo[par][:, cols], start=False, stop=True)
            last.then_inc(qq_ps, 1)

        def scores(b, par, j):
            n = (par + j) % 2
            m = tile_n(j)
            if j == 0:
                pe.wait_ge(qlo_sb, b + 1)
            for h in range(2):
                cols = slice(h * NQ, (h + 1) * NQ)
                for part in (k_hi, k_lo):
                    last = nc.tensor.matmul(ps[0:m, 2 * n + h, 0:NQ], part[par][:, j * TW:j * TW + m],
                                            q_s[par][:, cols], start=part is k_hi, stop=part is k_lo)
            last.then_inc(s_ps, 1)

        def values(b, par, j):
            n = (par + j) % 2
            m = tile_n(j)
            pe.wait_ge(sig_done, b * NT + j + 1)
            if j == 0:
                pe.wait_ge(o_sb, b)
            for h in range(2):
                last = nc.tensor.matmul(ps[h * C:(h + 1) * C, 6, 0:NQ], xs[par][0:m, j, 0, :], att[n][0:m, h, :],
                                        start=(j == 0), stop=(j == NT - 1))
            last.then_inc(av_done, 1)

        def back_waits(b, lag):
            if lag:
                pe.wait_ge(gate_sb, b - 1 + AHEAD)
            pe.wait_ge(o_sb, b + 1)

        def back(b):
            for t in range(NT):
                last = nc.tensor.transpose(ps[0:TW, 7, t * C:(t + 1) * C], o_t[:, t * TW:(t + 1) * TW],
                                           ident[0:C, 0:C])
            last.then_inc(ot_ps, 1)

        def norm_t(b, first=4):
            pe.wait_ge(xn2_ready, b + 1)
            if first == 6:
                pe.wait_ge(o_sb, NB)
                pe.wait_ge(gate_sb, b + AHEAD)
            for t in range(NT):
                n = tile_n(t)
                bank, o = divmod(t, 4)
                last = nc.tensor.transpose(ps[:, first + bank, o * TW:o * TW + n],
                                           xn2[0:n, t, :, :].rearrange("q k c -> q (k c)"), ident[0:n, 0:n])
            last.then_inc(x2t_ps, 1)

        def gates(b, lag=False):
            if lag:
                pe.wait_ge(h2_ready, b + 2)
            pe.wait_ge(x2_ready, b + 1)
            for t in range(NT):
                last = nc.tensor.matmul(ps[0:TW, 7, t * 2 * E:(t + 1) * 2 * E], x2_s[:, t * TW:(t + 1) * TW],
                                        gw_r[:].rearrange("d k e -> d (k e)"), start=True, stop=True)
            last.then_inc(gate_ps, 1)

        def dispatch_t(g, bank):
            pe.wait_ge(disp_ready, g + 1)
            for b in range(GB):
                last = nc.tensor.transpose(ps[0:NT * E, bank, b * TW:(b + 1) * TW],
                                           logit[:, g * GB + b, :, :].rearrange("q t e -> q (t e)"),
                                           ident[0:TW, 0:TW])
            last.then_inc(dt_ps, 1)

        def step(b, par, prep, tail, lag):
            scores(b, par, 0)
            scores(b, par, 1)
            if lag:
                norm_t(b - 2)
            values(b, par, 0)
            if tail:
                back_waits(b - 1, lag)
            scores(b, par, 2)
            if tail:
                back(b - 1)
            values(b, par, 1)
            scores(b, par, 3)
            if prep:
                key_t(b + 1, 1 - par, lag)
            values(b, par, 2)
            scores(b, par, 4)
            values(b, par, 3)
            scores(b, par, 5)
            if prep:
                query(b + 1, 1 - par)
            values(b, par, 4)
            scores(b, par, 6)
            if lag:
                gates(b - 2, True)
            values(b, par, 5)
            if not prep:
                pe.wait_ge(x2_ready, NB - 2)
                dispatch_t(0, 4)
            values(b, par, 6)

        key_t(0, 0, first=0)
        bands_t(NPAIR - 1)
        pe.wait_ge(act_const, 4)
        pe.wait_ge(dve_const, 4)
        query(0, 0, 0)
        window_sums(NPAIR - 1)
        pe.wait_ge(h_sb, NPAIR)
        step(0, 0, True, False, False)
        step(1, 1, True, True, False)
        with pe.Fori(0, 2) as i:
            step(i * 2 + 2, 0, True, True, True)
            step(i * 2 + 3, 1, True, True, True)
        step(6, 0, True, True, True)
        step(7, 1, False, True, True)

        pe.wait_ge(w_split, 1)
        def expert(c, e, first):
            k = e % 2
            if not (first and e < 2):
                pe.wait_ge(prod_done, c * E + e - 1)
            xc = x3[:, bass.ds(c * CH, CH)]
            for j in range(2):
                nc.tensor.matmul(ps[:, 2 * j + k, 0:CH], w_hi[j][:, e, :], xc, start=True, stop=False)
                last = nc.tensor.matmul(ps[:, 2 * j + k, 0:CH], w_lo[j][:, e, :], xc, start=False, stop=True)
            last.then_inc(h_ready, 1)

        def project(c, p, first):
            pe.wait_ge(prod_done, c * E + 2 * p + 2)
            if not (first and p < 2):
                pe.wait_ge(scale_done, c * NPE + p - 1)
            for k in range(2):
                e = 2 * p + k
                last = nc.tensor.matmul(ps[k * C:(k + 1) * C, 4 + p % 2, 0:CH], w3_s[:, e, :], prod[e % 4][:],
                                        start=True, stop=True)
            last.then_inc(out_done, 1)

        def collect(c):
            pe.wait_ge(add_done, c * 7 + 7)
            pe.wait_ge(fin_done, c + AHEAD)
            for j in range(4):
                last = nc.tensor.matmul(ps[0:YT, 6, j * C:(j + 1) * C], acc_f[:, j * YT:(j + 1) * YT], stack2[:],
                                        start=True, stop=True)
            last.then_inc(y_done, 1)

        def chunk(c, first=False, late=0):
            for p in range(NPE):
                expert(c, 2 * p, first)
                expert(c, 2 * p + 1, first)
                if first and p == 0:
                    norm_t(NB - 2, 6)
                if first and p == 1:
                    pe.wait_ge(dt_sb, 1)
                if first and p == 2:
                    gates(NB - 2)
                if first and p == 3:
                    back_waits(NB - 1, False)
                    pe.wait_ge(gate_sb, NB - 1 + AHEAD)
                    back(NB - 1)
                if late == 1 and p == 1:
                    gates(NB - 1)
                if late == 2 and p == 0:
                    dispatch_t(1, 7)
                if p > 0:
                    project(c, p - 1, first)
                elif not first:
                    project(c - 1, NPE - 1, False)
                if p == 2 and not first:
                    collect(c - 1)

        chunk(0, first=True)
        norm_t(NB - 1, 6)
        with pe.Fori(1, 2) as c:
            chunk(c, late=1)
        with pe.Fori(2, 3) as c:
            chunk(c, late=2)
        with pe.Fori(3, C_HALF) as c:
            chunk(c)
        pe.wait_ge(x3_stored, NB * 16 + DMA_AHEAD)
        with pe.Fori(C_HALF, NCH) as c:
            chunk(c)
        project(NCH - 1, NPE - 1, False)
        collect(NCH - 1)

    @block.vector
    def _(dve):
        steps = [0]

        class Chain:

            def __init__(self, base):
                self.base, self.n = base, 0

            def link(self, ins):
                self.n += 1
                ins.then_inc(dve_step, 1)
                dve.wait_ge(dve_step, self.base + self.n)

        tt, ts = nc.vector.tensor_tensor, nc.vector.tensor_scalar

        nc.vector.memset(qb[:, :, 0:8], 0.0)
        nc.vector.memset(qb[:, :, 8 + NW:QW], 0.0)
        nc.vector.memset(kx[:, :, L:KXW], 0.0)
        nc.vector.memset(sc_s[:, NW:NWP], 0.0)
        nc.vector.memset(v_sel[:], 0.0).then_inc(dve_const, 1)
        for e in range(E):
            last = nc.vector.memset(rank[:, e:e + 1], float(E - e))
        last.then_inc(dve_const, 1)
        dve.wait_ge(dve_const, 2)
        dve.wait_ge(tok_loaded, N_TOK_LOADS * 16)
        for k in range(2):
            for i in range(3):
                last = nc.vector.tensor_copy(v_sel[k * C:(k + 1) * C, i, 3 * k + i:3 * k + i + 1],
                                             v_col[k * C:(k + 1) * C, :])
        last.then_inc(dve_const, 1)
        def sums(p, i):
            if i == 0:
                dve.wait_ge(q_sb, p + 1)
                dve.wait_ge(k_sb, p + 1)
            for g in range(3):
                r, o = 3 * g + i, (3 * i + g) * QW
                dst = th[:, p % 2, o + r:o + r + KXW].rearrange("q (s w) -> q s w", w=WIN)
                q = qb[:, p, r:r + KXW].rearrange("q (s w) -> q s w", w=WIN)
                k = kx[:, p, :].rearrange("q (s w) -> q s w", w=WIN)[:, :, r:r + 1]
                last = tt(dst, q, k.broadcast_to([128, SEG, WIN]), ALU.add)
            last.then_inc(sum_done, 1)

        def softmax_top(p):
            dve.wait_ge(sct_ps, p + 1)
            if p:
                dve.wait_ge(band_ready, 2 * p)
            for b in range(2):
                for k in range(2):
                    n = 4 - k
                    src = ps[0:TW, 2 + k, 0:n * 96].rearrange("q (t g i) -> q t g i", t=n, g=3)
                    last = nc.vector.tensor_copy(
                        wt[:, b, 4 * k:4 * k + n, :].rearrange("q t (g i) -> q t g i", g=3),
                        src[:, :, :, 3 * b:3 * b + 3])
            last.then_inc(wt_copied, 1)
            dve.wait_ge(wt_copied, p + 1)
            chain.link(nc.vector.tensor_reduce(wt_max[:], wt_rows, AX.X, ALU.max))
            tt(wt_rows, wt_rows, wt_max[:].unsqueeze(2).broadcast_to([TW, 2 * NT, WIN]), ALU.subtract
               ).then_inc(shifted, 1)

        def softmax_end(p):
            dve.wait_ge(exp_done, p + 1)
            chain.link(nc.vector.tensor_reduce(wt_sum[:], wt_rows, AX.X, ALU.add))
            chain.link(nc.vector.reciprocal(wt_sum[:], wt_sum[:]))
            tt(wt_rows, wt_rows, wt_sum[:].unsqueeze(2).broadcast_to([TW, 2 * NT, WIN]), ALU.mult
               ).then_inc(wt_ready, 1)

        def mean_a(p):
            dve.wait_ge(h_sb, p + 1)
            h = h_all[:, 2 * p:2 * p + 2, :, :].rearrange("q b t c -> q (b t) c")
            chain.link(nc.vector.tensor_reduce(ln_s[:, 1, :], h, AX.X, ALU.add))
            ts(ln_s[:, 0, :], ln_s[:, 1, :], 1.0 / C, None, ALU.mult).then_inc(mean_ready, 1)

        def var_a(p):
            dve.wait_ge(sq_ready, p + 1)
            chain.link(nc.vector.tensor_reduce(ln_s[:, 1, :], ln_sq[:], AX.X, ALU.add))
            ts(ln_s[:, 2, :], ln_s[:, 1, :], 1.0 / C, 1e-5, ALU.mult, ALU.add).then_inc(var_ready, 1)

        def normed_a(p):
            dve.wait_ge(rstd_ready, p + 1)
            tt(xn_all[:, 2 * p:2 * p + 2, :, :].rearrange("q b t c -> q (b t) c"), ln_c[:],
               ln_s[:, 3, :].unsqueeze(2).broadcast_to([TW, 2 * NT, C]), ALU.mult).then_inc(xn_ready, 1)

        wt_rows = wt[:].rearrange("q b t r -> q (b t) r")
        chain = Chain(0)
        for i in range(3):
            sums(0, i)
        for p in range(NPAIR):
            more = p + 1 < NPAIR
            if p > 0:
                softmax_top(p - 1)
                softmax_end(p - 1)
            if more and p > 0:
                dve.wait_ge(sc_ps, p)
            if more:
                sums(p + 1, 0)
            if p > 2:
                var_a(p - 3)
            if more:
                sums(p + 1, 1)
            if p > 2:
                normed_a(p - 3)
            if p > 1:
                mean_a(p - 2)
            if more:
                sums(p + 1, 2)
            if p == NPAIR - 2:
                dve.wait_ge(act_const, 4)
                tt(qw_r[C:128, :], qw_f[C:128, :], qw_r[C:128, :].bitcast(F32), ALU.subtract)
                tt(gw_r[:, 1, :], gw_f[:], gw_r[:, 0, :].bitcast(F32), ALU.subtract).then_inc(dve_const, 1)
                dve.wait_ge(sum_done, NPAIR * 3)
                for par in range(2):
                    nc.vector.memset(k_hi[par][:, NW:NWP].bitcast(F32), 0.0)
                    last = nc.vector.memset(k_lo[par][:, NW:NWP].bitcast(F32), 0.0)
                last.then_inc(sums_read, 1)
        softmax_top(NPAIR - 1)
        softmax_end(NPAIR - 1)
        var_a(NPAIR - 3)
        normed_a(NPAIR - 3)
        mean_a(NPAIR - 2)

        def pads():
            nc.vector.memset(x2_s[:, NW:NWP].bitcast(F32), 0.0)
            nc.vector.memset(x3[:, TOK:TOKP].bitcast(F32), 0.0)
            nc.vector.memset(zrow[:], 0.0)
            nc.vector.memset(o_t[:, NW:NWP], 0.0).then_inc(b_init, 1)

        def key_lo(b, par, bank=4):
            dve.wait_ge(khi_sb, b + 1)
            tt(k_lo[par][:, 0:BK], ps[:, bank, 0:BK], k_hi[par][:, 0:BK].bitcast(F32), ALU.subtract)
            tt(k_lo[par][:, BK:NW], ps[:, bank + 1, 0:NW - BK], k_hi[par][:, BK:NW].bitcast(F32), ALU.subtract
               ).then_inc(klo_sb, 1)

        def query_lo(b, par, bank=4):
            dve.wait_ge(qhi_sb, b + 1)
            low = q_s[par][C:128, :].rearrange("q (h n) -> q h n", h=2)
            tt(low, ps[C:128, bank:bank + 2, 0:NQ], low.bitcast(F32), ALU.subtract).then_inc(qlo_sb, 1)

        def attended(b):
            dve.wait_ge(av_done, (b + 1) * NT)
            dve.wait_ge(ot_ps, b + AHEAD)
            nc.vector.tensor_copy(o_t[:, 0:NQ], ps[0:C, 6, 0:NQ])
            nc.vector.tensor_copy(o_t[:, NQ:NW], ps[C:128, 6, 0:NW - NQ]).then_inc(o_sb, 1)

        def residual(b, chain):
            dve.wait_ge(ot_ps, b + 1 + AHEAD)
            dve.wait_ge(h2_stored, b * 32 + DMA_AHEAD)
            tt(h2_s[:], ps[0:TW, 7, 0:NT * C].rearrange("q (t c) -> q t c", c=C),
               h_all[:, bass.ds(b, 1), :, :].rearrange("q a t c -> q (a t) c"), ALU.add).then_inc(h2_ready, 1)
            dve.wait_ge(h2_ready, b + 1)
            chain.link(nc.vector.tensor_reduce(bn_s[:, 1, :], h2_s[:], AX.X, ALU.add))
            ts(bn_s[:, 0, :], bn_s[:, 1, :], 1.0 / C, None, ALU.mult).then_inc(mean2, 1)

        def variance(b, chain):
            dve.wait_ge(sq2, b + 1)
            chain.link(nc.vector.tensor_reduce(bn_s[:, 1, :], bn_sq[:], AX.X, ALU.add))
            ts(bn_s[:, 2, :], bn_s[:, 1, :], 1.0 / C, 1e-5, ALU.mult, ALU.add).then_inc(var2, 1)

        def x2_lo(b, bank=4):
            dve.wait_ge(x2hi_sb, b + 1)
            tt(x2_s[C:128, 0:BK], ps[C:128, bank, 0:BK], x2_s[C:128, 0:BK].bitcast(F32), ALU.subtract)
            tt(x2_s[C:128, BK:NW], ps[C:128, bank + 1, 0:NW - BK], x2_s[C:128, BK:NW].bitcast(F32), ALU.subtract
               ).then_inc(x2_ready, 1)

        def logits(b, chain):
            lg = logit[:, bass.ds(b, 1), :, :].rearrange("q a t e -> q (a t) e")
            dve.wait_ge(gate_ps, b + 1 + AHEAD)
            parts = ps[0:TW, 7, 0:NT * 2 * E].rearrange("q (t k e) -> q k t e", k=2, e=E)
            chain.link(tt(lg, parts[:, 0], gb_row[:].unsqueeze(1).broadcast_to([TW, NT, E]), ALU.add))
            tt(lg, parts[:, 1], lg, ALU.add).then_inc(gate_sb, 1)

        def route(g, part, chain):
            over = lambda v: v.unsqueeze(2).broadcast_to([TW, GB * NT, E])
            lg = logit[:, g * GB:(g + 1) * GB, :, :].rearrange("q b t e -> q (b t) e")
            rk = rank[:].unsqueeze(1).broadcast_to([TW, GB * NT, E])
            if part == 0:
                chain.link(nc.vector.tensor_reduce(r_m[:, 0, :], lg, AX.X, ALU.max))
                chain.link(tt(lg, lg, over(r_m[:, 0, :]), ALU.subtract))
                chain.link(nc.vector.scalar_tensor_tensor(r_b[:], lg, 0.0, rk, ALU.is_equal, ALU.mult))
            elif part == 1:
                chain.link(nc.vector.tensor_reduce(r_m[:, 1, :], r_b[:], AX.X, ALU.max))
                chain.link(tt(r_b[:], r_b[:], over(r_m[:, 1, :]), ALU.is_equal))
                chain.link(nc.vector.scalar_tensor_tensor(r_a[:], r_b[:], -BIG, lg, ALU.mult, ALU.add))
            elif part == 2:
                chain.link(nc.vector.tensor_reduce(r_m[:, 2, :], r_a[:], AX.X, ALU.max))
                chain.link(tt(r_a[:], r_a[:], over(r_m[:, 2, :]), ALU.is_equal))
                chain.link(tt(r_a[:], r_a[:], rk, ALU.mult))
            else:
                chain.link(nc.vector.tensor_reduce(r_m[:, 3, :], r_a[:], AX.X, ALU.max))
                tt(r_a[:], r_a[:], over(r_m[:, 3, :]), ALU.is_equal).then_inc(routed, 1)

        def dispatch(g, chain):
            dve.wait_ge(rw_ready, g + 1)
            dve.wait_ge(routed, g + 1)
            over = lambda v: v.unsqueeze(2).broadcast_to([TW, GB * NT, E])
            tt(r_b[:], r_b[:], over(r_w[:, 0, :]), ALU.mult)
            chain.link(tt(r_a[:], r_a[:], over(r_w[:, 1, :]), ALU.mult))
            tt(logit[:, g * GB:(g + 1) * GB, :, :].rearrange("q b t e -> q (b t) e"), r_b[:], r_a[:], ALU.add
               ).then_inc(disp_ready, 1)

        TAIL_LINKS, B_LINKS = 2, 3
        b_first = NPAIR * 5

        def step(b, par, prep, tail, lag, chain=None):
            if chain is None:
                chain = Chain(b_first if not lag else (b - 2) * B_LINKS + b_first + TAIL_LINKS)
                routing = False
            else:
                routing = True
            if tail:
                attended(b - 1)
            if routing and not prep:
                route(0, 3, chain)
            if lag:
                x2_lo(b - 2)
            if tail:
                residual(b - 1, chain)
            if routing and prep:
                dve.wait_ge(gate_sb, GB + AHEAD)
                route(0, 0, chain)
            if prep:
                key_lo(b + 1, 1 - par)
            if tail:
                variance(b - 1, chain)
            if routing and prep:
                route(0, 1, chain)
            if routing and not prep:
                dispatch(0, chain)
            if prep:
                query_lo(b + 1, 1 - par)
            if lag:
                logits(b - 2, chain)
            if routing and prep:
                route(0, 2, chain)

        key_lo(0, 0, 0)
        query_lo(0, 0, 0)
        var_a(NPAIR - 2)
        normed_a(NPAIR - 2)
        mean_a(NPAIR - 1)
        pads()
        key_lo(1, 1)
        var_a(NPAIR - 1)
        query_lo(1, 1)
        normed_a(NPAIR - 1)
        for k in range(2):
            last = tt(w_lo[k][:].rearrange("d e h -> d (e h)"), w_f[k][:],
                      w_hi[k][:].rearrange("d e h -> d (e h)").bitcast(F32), ALU.subtract)
        last.then_inc(w_split, 1)
        assert chain.n == b_first
        step(1, 1, True, True, False)
        with dve.Fori(0, 2) as i:
            step(i * 2 + 2, 0, True, True, True)
            step(i * 2 + 3, 1, True, True, True)
        chain = Chain(b_first + TAIL_LINKS + 4 * B_LINKS)
        step(6, 0, True, True, True, chain)
        step(7, 1, False, True, True, chain)
        attended(NB - 1)

        def product(c, e, first):
            dve.wait_ge(sil_done, c * E + e + 1)
            if not (first and e < 4):
                dve.wait_ge(out_done, c * NPE + e // 2 - 1)
            tt(prod[e % 4][:], sil[e % 2][:], ps[:, 2 + e % 2, 0:CH], ALU.mult).then_inc(prod_done, 1)

        def scale(c, p, first):
            dve.wait_ge(out_done, c * NPE + p + 1)
            dve.wait_ge(db_loaded[p % 4], (c * 2 + p // 4 + 1) * 16)
            if p >= 3:
                dve.wait_ge(add_done, c * 7 + p - 2)
            elif not first:
                dve.wait_ge(add_done, c * 7)
            dst = acc if p == 0 else res[p % 2]
            tt(dst[:], ps[:, 4 + p % 2, 0:CH], db[p % 4][:], ALU.mult).then_inc(scale_done, 1)

        def finish(c, first):
            dve.wait_ge(y_done, c + 1)
            dve.wait_ge(h2_loaded, (c + 1) * 16)
            if not first:
                dve.wait_ge(out_stored, c * 16 + DMA_AHEAD)
            tt(fin[:], ps[0:YT, 6, 0:4 * C].rearrange("q (j c) -> q j c", c=C), h2_c[:], ALU.add
               ).then_inc(fin_done, 1)

        def chunk(c, first=False, late=False):
            for p in range(NPE):
                product(c, 2 * p, first)
                product(c, 2 * p + 1, first)
                if p > 0:
                    scale(c, p - 1, first)
                elif not first:
                    scale(c - 1, NPE - 1, False)
                if first and p == 1:
                    x2_lo(NB - 2, 6)
                if first and p == 2:
                    logits(NB - 2, chain)
                if first and p == 3:
                    residual(NB - 1, chain)
                if first and p == 5:
                    variance(NB - 1, chain)
                if late and p == 0:
                    x2_lo(NB - 1, 6)
                if late and p == 1:
                    logits(NB - 1, chain)
                    dve.wait_ge(gate_sb, NB + AHEAD)
                if late and 2 <= p <= 5:
                    route(1, p - 2, chain)
                if late and p == 7:
                    dispatch(1, chain)
                if p == 3 and not first:
                    finish(c - 1, False)

        chunk(0, first=True)
        chunk(1, late=True)
        with dve.Fori(2, NCH) as c:
            chunk(c)
        scale(NCH - 1, NPE - 1, False)
        finish(NCH - 1, False)

    ctx.close()


_INS = ["x", "L0_tok_W_qry", "L0_tok_W_key", "L0_tok_v", "L0_tok_b", "L0_attn_q_weight", "L0_ffn_gate_w",
        "L0_ffn_gate_b", "L0_ffn_w1", "L0_ffn_w2", "L0_ffn_w3"]


def kernel(**inputs):
    import numpy as _np
    import concourse.bacc as _bacc
    from concourse import mybir as _mybir
    from concourse.bass_utils import run_bass_kernel_spmd as _run

    nc = _bacc.Bacc("TRN2", target_bir_lowering=False, num_devices=1)
    arrays, args = {}, []
    for name in _INS:
        a = _np.ascontiguousarray(inputs[name])
        arrays[f"in_{name}"] = a
        args.append(nc.dram_tensor(f"in_{name}", a.shape, _mybir.dt.from_np(a.dtype), kind="ExternalInput").ap())
    out = nc.dram_tensor("out_0", (NB, NW, C), _mybir.dt.float32, kind="ExternalOutput").ap()
    build(nc, *args, out)
    r = _run(nc, [arrays], core_ids=[0])
    return r.results[0]["out_0"]
```

```python
from contextlib import ExitStack

import concourse.bass as bass
from concourse import mybir

F32 = mybir.dt.float32
F32R = mybir.dt.float32r
ALU = mybir.AluOpType
ACT = mybir.ActivationFunctionType
AX = mybir.AxisListType

NB, L, C = 8, 750, 64
WIN = 9
NW = L - WIN + 1
TW, NT = 108, 7
TL = NW - (NT - 1) * TW
KW = TW + WIN - 1
NPAIR = NB // 2
NWP = NT * TW
HALF = NW // 2
NQ = 372
BK = 4 * TW
SEG = 84
QW = 764
KXW = SEG * WIN
E, HID = 16, 128
TOK = NB * NW
CH, NCH = 496, 12
TOKP = CH * NCH
C_HALF = 5
YT = CH // 4
GB = NB // 2
NPE = E // 2
BIG = 3.0e38
AHEAD, DMA_AHEAD = 1, 16


def tile_n(t):
    return TW if t < NT - 1 else TL


def build(nc, x, wq_tok, wk_tok, v_tok, b_tok, q_weight, gate_w, gate_b, w1, w2, w3, out):
    ctx = ExitStack()
    place = [16512]

    def at(name, shape, dt=F32, offset=None):
        size = 4
        for n in shape[1:]:
            size *= n
        if offset is None:
            offset = place[0]
            place[0] += (size + 31) // 32 * 32
        return nc.alloc_sbuf_tensor_at(name, list(shape), dt, offset=offset)

    ident = at("ident", [128, 128])
    stack2 = at("stack2", [128, C])
    band = at("band", [TW, 13 * WIN])
    wq_bd = at("wq_bd", [128, 128])
    wk_bd = at("wk_bd", [128, 128])
    v_col = at("v_col", [128, 1])
    b_col = at("b_col", [128, 1])
    v_sel = at("v_sel", [128, 3, 32])
    qw_f = at("qw_f", [128, 128])
    qw_r = at("qw_r", [128, 128], F32R)
    gw_f = at("gw_f", [128, E])
    gw_r = at("gw_r", [128, 2, E], F32R)
    gb_row = at("gb_row", [TW, E])
    rank = at("rank", [TW, E])
    neg_half = at("neg_half", [TW, 2 * NT])
    w_f = [at(f"w{k}_f", [128, E * HID]) for k in (1, 2)]
    w_hi = [at(f"w{k}_hi", [128, E, HID], F32R) for k in (1, 2)]
    w_lo = [at(f"w{k}_lo", [128, E, HID], F32R) for k in (1, 2)]
    w3_s = at("w3_s", [HID, E, C])
    h_all = at("h_all", [TW, NB, NT, C])
    xn_all = at("xn_all", [TW, NB, NT, C])

    xk = at("xk", [KW, NPAIR, NT, 2, C])
    a_base = place[0]
    x_t = at("x_t", [128, 2, L])
    qb = at("qb", [128, NPAIR, QW])
    kx = at("kx", [128, NPAIR, KXW])
    sc_s = at("sc_s", [96, NWP])
    wt = at("wt", [TW, 2, NT, WIN])
    wt_max = at("wt_max", [TW, 2 * NT])
    wt_sum = at("wt_sum", [TW, 2 * NT])
    band_a = at("band_a", [TW, 2 * NT, 13 * WIN])
    band_t = at("band_t", [KW, 2 * NT, TW])
    ln_c = at("ln_c", [TW, 2 * NT, C])
    ln_sq = at("ln_sq", [TW, 2 * NT, C])
    ln_s = at("ln_s", [TW, 2, 4, 2 * NT])
    a_end = place[0]
    t_base = place[0]
    th = at("th", [128, 2, WIN * QW])
    t_end = place[0]

    place[0] = a_base
    even = []

    def pair(name, shape, dt):
        even.append(place[0])
        return [at(f"{name}{p}", shape, dt) for p in range(2)]

    xs = pair("xs", [TW, NT, 2, C], F32)
    k_hi = pair("k_hi", [128, NWP], F32R)
    k_lo = pair("k_lo", [128, NWP], F32R)
    q_s = pair("q_s", [128, 2 * NQ], F32R)
    tail_base = place[0] = max(place[0], even[3] + 6 * CH * 4)
    o_t = at("o_t", [C, NWP])
    assert place[0] <= t_base
    bn_c = at("bn_c", [TW, NT, C])
    assert place[0] <= a_end
    place[0] = t_base
    x3 = at("x3", [128, TOKP], F32R)
    h2_s = at("h2_s", [TW, NT, C])
    xn2 = at("xn2", [TW, NT, 2, C])
    x2_s = at("x2_s", [128, NWP], F32R)
    bn_sq = at("bn_sq", [TW, NT, C])
    bn_s = at("bn_s", [TW, 4, NT])
    r_a = at("r_a", [TW, GB * NT, E])
    r_b = at("r_b", [TW, GB * NT, E])
    r_m = at("r_m", [TW, 4, GB * NT])
    logit = at("logit", [TW, NB, NT, E])
    r_w = at("r_w", [TW, 2, GB * NT])
    zrow = at("zrow", [E, C])
    d_t = at("d_t", [NT * E, NB, TW])
    att = [at(f"att{p}", [TW, 2, NQ]) for p in range(2)]
    assert place[0] <= t_end
    even.append(tail_base)
    db, rest = [], {}
    for k, names in enumerate((("h2_c", "fin"), ("sil0", "sil1"), ("prod0", "prod1"),
                               ("prod2", "prod3", "res0", "res1", "acc"))):
        place[0] = even[k]
        db.append(at(f"db{k}", [128, CH]))
        for name in names:
            rest[name] = at(name, [YT, 4, C] if name in ("h2_c", "fin") else [128, CH])
        if k == 0:
            acc_f = at("acc_f", [128, CH])
        assert place[0] <= even[k + 1]
    sil, res = ([rest[f"{name}{k}"] for k in range(2)] for name in ("sil", "res"))
    prod = [rest[f"prod{k}"] for k in range(4)]
    acc, h2_c, fin = rest["acc"], rest["h2_c"], rest["fin"]
    assert place[0] <= tail_base

    h2_d = nc.dram_tensor("h2_d", [TOKP, C], F32).ap()
    dt_d = nc.dram_tensor("dt_d", [E, TOKP], F32).ap()

    ps = ctx.enter_context(nc.psum_tensor("ps", [128, 8, 512], F32))

    def sem(name):
        return ctx.enter_context(nc.semaphore(name))

    tok_loaded, w_loaded, pool_const, dve_const, act_const = (
        sem(n) for n in ("tok_loaded", "w_loaded", "pool_const", "dve_const", "act_const"))
    sums_read = sem("sums_read")
    w_split = sem("w_split")
    bias_loaded = sem("bias_loaded")
    xn_last = sem("xn_last")
    xt_first = sem("xt_first")
    x_loaded = [sem(f"x_loaded{p}") for p in range(NPAIR)]
    xt_ps, xt_sb, q_ps, q_sb, k_ps, k_sb = (sem(n) for n in ("xt_ps", "xt_sb", "q_ps", "q_sb", "k_ps", "k_sb"))
    sum_done, tanh_done, sc_ps, sc_sb, sct_ps, wt_copied = (
        sem(n) for n in ("sum_done", "tanh_done", "sc_ps", "sc_sb", "sct_ps", "wt_copied"))
    shifted, exp_done, wt_ready, band_ready, bt_ps = (
        sem(n) for n in ("shifted", "exp_done", "wt_ready", "band_ready", "bt_ps"))
    bt_sb, h_ps, h_sb = (sem(n) for n in ("bt_sb", "h_ps", "h_sb"))
    mean_ready, sq_ready, var_ready, rstd_ready, xn_ready = (
        sem(n) for n in ("mean_ready", "sq_ready", "var_ready", "rstd_ready", "xn_ready"))
    xs_loaded, kt_ps, khi_sb, klo_sb, qq_ps, qhi_sb, qlo_sb = (
        sem(n) for n in ("xs_loaded", "kt_ps", "khi_sb", "klo_sb", "qq_ps", "qhi_sb", "qlo_sb"))
    s_ps, sig_done, av_done, o_sb, ot_ps, h2_ready, h2_stored = (
        sem(n) for n in ("s_ps", "sig_done", "av_done", "o_sb", "ot_ps", "h2_ready", "h2_stored"))
    mean2, sq2, var2, rstd2, xn2_ready, x2t_ps, x2hi_sb, x2_ready, x3_stored = (
        sem(n) for n in ("mean2", "sq2", "var2", "rstd2", "xn2_ready", "x2t_ps", "x2hi_sb", "x2_ready", "x3_stored"))
    gate_ps, gate_sb, b_init, routed, rw_ready, disp_ready, dt_ps, dt_sb, dt_stored = (
        sem(n) for n in ("gate_ps", "gate_sb", "b_init", "routed", "rw_ready", "disp_ready", "dt_ps", "dt_sb",
                         "dt_stored"))
    pad_stored = sem("pad_stored")
    h_ready, sil_done, prod_done, out_done, scale_done, add_done, y_done, fin_done = (
        sem(n) for n in ("h_ready", "sil_done", "prod_done", "out_done", "scale_done", "add_done", "y_done",
                         "fin_done"))
    db_loaded = [sem(f"db_loaded{k}") for k in range(4)]
    h2_loaded, out_stored = sem("h2_loaded"), sem("out_stored")
    dve_step, pool_step = sem("dve_step"), sem("pool_step")

    out_rows = out.rearrange("b n c -> (b n) c")
    N_TOK_LOADS, N_W_LOADS = 2 * 2, 2 * 5 + 2

    block = ctx.enter_context(nc.Block())

    @block.sync
    def _(sp):
        for p in range(NPAIR):
            for b in range(2):
                xb = x[2 * p + b]
                rows = bass.AP(xb.tensor, xb.offset, [[C, KW], [TW * C, NT - 1], [1, C]])
                sp.dma_start(xk[:, p, 0:NT - 1, b, :], rows).then_inc(x_loaded[p], 16)
            rows = bass.AP(x.tensor, x.offset + (2 * p * L + (NT - 1) * TW) * C, [[C, TL + WIN - 1], [L * C, 2], [1, C]])
            sp.dma_start(xk[0:TL + WIN - 1, p, NT - 1, :, :], rows).then_inc(x_loaded[p], 16)

        halves = (slice(0, C), slice(C, 128))

        def load(dst, src):
            sp.dma_start(dst, src).then_inc(w_loaded, 16)

        for half in halves:
            load(qw_f[half, 0:C], q_weight)
            load(qw_f[half, C:128], q_weight)
            load(gw_f[half, :], gate_w)
            for w, dst in ((w1, w_f[0]), (w2, w_f[1])):
                load(dst[half, :].rearrange("d (e h) -> d e h", h=HID), w.rearrange("e d h -> d e h"))
        load(gb_row[:], gate_b.rearrange("(a e) -> a e", a=1).broadcast_to([TW, E]))
        load(w3_s[:], w3.rearrange("e h o -> h e o"))

        def stage_in(b, par):
            sp.wait_ge(xs_loaded, b * 32)
            for k in range(2):
                sp.dma_start(xs[par][:, :, k, :], xn_all[:, bass.ds(b, 1), :, :].rearrange("p a t c -> p (a t) c")
                             ).then_inc(xs_loaded, 16)

        def store_h2(b):
            sp.wait_ge(h2_ready, b + 1)
            rows = h2_d[bass.ds(b * NW, (NT - 1) * TW), :].rearrange("(t p) c -> p t c", p=TW)
            sp.dma_start(rows, h2_s[:, 0:NT - 1, :]).then_inc(h2_stored, 16)
            sp.dma_start(h2_d[bass.ds(b * NW + (NT - 1) * TW, TL), :], h2_s[0:TL, NT - 1, :]).then_inc(h2_stored, 16)

        def store_x3(b):
            sp.wait_ge(x2_ready, b + 1)
            sp.dma_start(x3[:, bass.ds(b * NW, NW)].bitcast(F32), x2_s[:, 0:NW].bitcast(F32)).then_inc(x3_stored, 16)

        def step(b, par, more, tail, lag):
            if lag:
                store_x3(b - 2)
            if tail:
                store_h2(b - 1)
            if more:
                sp.wait_ge(av_done, (b + 1) * NT)
                stage_in(b + 2, par)

        sp.wait_ge(sums_read, 1)
        sp.wait_ge(xn_ready, 1)
        sp.wait_ge(k_ps, NPAIR)
        stage_in(0, 0)
        stage_in(1, 1)
        sp.wait_ge(b_init, 1)
        sp.dma_start(h2_d[TOK:TOKP, :], zrow[0:TOKP - TOK, :]).then_inc(pad_stored, 16)
        sp.dma_start(dt_d[:, TOK:TOKP], zrow[:, 0:TOKP - TOK]).then_inc(pad_stored, 16)
        sp.wait_ge(xn_ready, 2)
        step(0, 0, True, False, False)
        step(1, 1, True, True, False)
        sp.wait_ge(xn_ready, NPAIR - 1)
        sp.wait_ge(xn_last, 1)
        with sp.Fori(0, 2) as i:
            step(i * 2 + 2, 0, True, True, True)
            step(i * 2 + 3, 1, True, True, True)
        step(6, 0, False, True, True)
        step(7, 1, False, True, True)

        def store_dt(b):
            rows = bass.AP(dt_d.tensor, dt_d.offset + b * NW, [[TW, NT - 1], [TOKP, E], [1, TW]])
            sp.dma_start(rows, d_t[0:(NT - 1) * E, b, :]).then_inc(dt_stored, 16)
            sp.dma_start(dt_d[:, b * NW + (NT - 1) * TW:(b + 1) * NW],
                         d_t[(NT - 1) * E:NT * E, b, 0:TL]).then_inc(dt_stored, 16)

        def load_db(c, p):
            src = dt_d[2 * p:2 * p + 2, bass.ds(c * CH, CH)].unsqueeze(1).broadcast_to([2, C, CH])
            sp.dma_start(db[p % 4][:], src).then_inc(db_loaded[p % 4], 16)

        def load_h2(c):
            rows = h2_d[bass.ds(c * CH, CH), :].rearrange("(j p) c -> p j c", p=YT)
            sp.dma_start(h2_c[:, :, :], rows).then_inc(h2_loaded, 16)

        def chunk(c, late=False):
            for p in range(NPE):
                sp.wait_ge(scale_done, c * NPE + p - 3)
                load_db(c, p)
                if late and p == 4:
                    sp.wait_ge(dt_sb, 2)
                    for b in range(GB, NB):
                        store_dt(b)
                if p == 6:
                    sp.wait_ge(fin_done, c + AHEAD)
                    sp.dma_start(out_rows[bass.ds((c - 1) * CH, CH), :].rearrange("(j p) c -> p j c", p=YT),
                                 fin[:, :, :]).then_inc(out_stored, 16)
                    load_h2(c)

        sp.wait_ge(dt_sb, 1)
        store_dt(0)
        sp.wait_ge(dt_stored, 2 * 16)
        sp.wait_ge(h2_stored, (NB - 1) * 32 + DMA_AHEAD)
        for p in range(4):
            load_db(0, p)
        for b in range(1, GB):
            store_dt(b)
        store_x3(NB - 2)
        load_h2(0)
        for p in range(4, NPE):
            sp.wait_ge(scale_done, p - 3)
            if p == NPE - 1:
                store_h2(NB - 1)
            load_db(0, p)
        sp.wait_ge(dt_stored, GB * 2 * 16)
        with sp.Fori(1, 2) as c:
            chunk(c)
        store_x3(NB - 1)
        with sp.Fori(2, 3) as c:
            chunk(c)
        with sp.Fori(3, 4) as c:
            chunk(c, late=True)
        with sp.Fori(4, C_HALF) as c:
            chunk(c)
        sp.wait_ge(dt_stored, NB * 2 * 16)
        sp.wait_ge(pad_stored, 32)
        sp.wait_ge(h2_stored, NB * 32 + DMA_AHEAD)
        with sp.Fori(C_HALF, NCH) as c:
            chunk(c)
        sp.wait_ge(fin_done, NCH + AHEAD)
        base = (NCH - 1) * CH
        sp.dma_start(out_rows[base:base + 3 * YT, :].rearrange("(j p) c -> p j c", p=YT),
                     fin[:, 0:3, :]).then_inc(out_stored, 16)
        sp.dma_start(out_rows[base + 3 * YT:TOK, :], fin[0:TOK - base - 3 * YT, 3, :]).then_inc(out_stored, 16)
        sp.wait_ge(out_stored, (NCH + 1) * 16 + DMA_AHEAD)

    @block.gpsimd
    def _(pool):
        for s in (ot_ps, x2t_ps, gate_sb,
                  gate_ps, fin_done):
            pool.sem_inc(s, AHEAD)
        for s in (h2_stored, x3_stored, out_stored):
            pool.sem_inc(s, DMA_AHEAD)
        nc.gpsimd.memset(wq_bd[:], 0.0).then_inc(pool_const, 1)
        nc.gpsimd.memset(wk_bd[:], 0.0).then_inc(pool_const, 1)
        nc.gpsimd.memset(ident[:], 0.0).then_inc(pool_const, 1)
        nc.gpsimd.memset(stack2[:], 0.0).then_inc(pool_const, 1)
        nc.gpsimd.memset(band[:], 1.0).then_inc(pool_const, 1)
        nc.gpsimd.memset(neg_half[:], -0.5).then_inc(pool_const, 1)
        pool.wait_ge(pool_const, 6)
        nc.gpsimd.affine_select(out=ident[:], in_=ident[:], compare_op=ALU.not_equal, fill=1.0, base=0,
                                pattern=[[-1, 128]], channel_multiplier=1).then_inc(pool_const, 1)
        nc.gpsimd.affine_select(out=stack2[:], in_=stack2[:], compare_op=ALU.not_equal, fill=1.0, base=0,
                                pattern=[[-1, C]], channel_multiplier=1).then_inc(pool_const, 1)
        nc.gpsimd.affine_select(out=band[:], in_=band[:], compare_op=ALU.is_ge, fill=0.0, base=0,
                                pattern=[[1, 13 * WIN]], channel_multiplier=-1).then_inc(pool_const, 1)
        pool.wait_ge(pool_const, 9)
        nc.gpsimd.affine_select(out=stack2[:], in_=stack2[:], compare_op=ALU.not_equal, fill=1.0, base=-C,
                                pattern=[[-1, C]], channel_multiplier=1).then_inc(pool_const, 1)
        nc.gpsimd.affine_select(out=band[:], in_=band[:], compare_op=ALU.is_ge, fill=0.0, base=WIN - 1,
                                pattern=[[-1, 13 * WIN]], channel_multiplier=1).then_inc(pool_const, 1)

        def norm_a(p):
            h = h_all[:, bass.ds(p * 2, 2), :, :].rearrange("q b t c -> q (b t) c")
            pool.wait_ge(mean_ready, p + 1)
            if p:
                pool.wait_ge(xn_ready, p)
            nc.gpsimd.tensor_tensor(ln_c[:], h, ln_s[:, p % 2, 0, :].unsqueeze(2).broadcast_to([TW, 2 * NT, C]),
                                    ALU.subtract).then_inc(pool_step, 1)
            pool.wait_ge(pool_step, p + 1)
            nc.gpsimd.tensor_tensor(ln_sq[:], ln_c[:], ln_c[:], ALU.mult).then_inc(sq_ready, 1)

        def bands(p):
            pool.wait_ge(wt_ready, p + 1)
            if p:
                pool.wait_ge(bt_ps, p * 4)
            m = band[:].rearrange("q (u r) -> q u r", r=WIN).unsqueeze(1).broadcast_to([TW, NT, 13, WIN])
            for b in range(2):
                f = wt[:, b, :, :].unsqueeze(2).broadcast_to([TW, NT, 13, WIN])
                nc.gpsimd.tensor_tensor(band_a[:, b * NT:(b + 1) * NT, :].rearrange("q n (u r) -> q n u r", r=WIN),
                                        f, m, ALU.mult).then_inc(band_ready, 1)

        def rstd_a(p):
            pool.wait_ge(var_ready, p + 1)
            nc.gpsimd.tensor_tensor(ln_s[:, p % 2, 3, :], ln_s[:, p % 2, 2, :], neg_half[:], ALU.pow).then_inc(rstd_ready, 1)

        for p in range(NPAIR):
            if p == 2:
                norm_a(0)
                rstd_a(0)
            bands(p)
        for p in range(1, NPAIR - 1):
            norm_a(p)
            rstd_a(p)
        norm_a(NPAIR - 1)

        def centre(b):
            pool.wait_ge(mean2, b + 1)
            nc.gpsimd.tensor_tensor(bn_c[:], h2_s[:], bn_s[:, 0, :].unsqueeze(2).broadcast_to([TW, NT, C]),
                                    ALU.subtract).then_inc(pool_step, 1)
            pool.wait_ge(pool_step, b + NPAIR + 1)
            nc.gpsimd.tensor_tensor(bn_sq[:], bn_c[:], bn_c[:], ALU.mult).then_inc(sq2, 1)

        def normed(b):
            pool.wait_ge(var2, b + 1)
            nc.gpsimd.tensor_tensor(bn_s[:, 3, :], bn_s[:, 2, :], neg_half[:, 0:NT], ALU.pow).then_inc(rstd2, 1)
            pool.wait_ge(rstd2, b + 1)
            pool.wait_ge(x2t_ps, b + AHEAD)
            nc.gpsimd.tensor_tensor(xn2[:], bn_c[:].unsqueeze(2).broadcast_to([TW, NT, 2, C]),
                                    bn_s[:, 3, :].unsqueeze(2).unsqueeze(3).broadcast_to([TW, NT, 2, C]),
                                    ALU.mult).then_inc(xn2_ready, 1)

        centre(0)
        normed(0)
        rstd_a(NPAIR - 1)
        pool.wait_ge(rstd_ready, NPAIR)
        last_pair = xn_all[:, NB - 2:NB, :, :].rearrange("q b t c -> q (b t) c")
        nc.gpsimd.tensor_tensor(last_pair, ln_c[:], ln_s[:, (NPAIR - 1) % 2, 3, :].unsqueeze(2).broadcast_to(
            [TW, 2 * NT, C]), ALU.mult).then_inc(xn_last, 1)
        with pool.Fori(1, NB - 1) as b:
            centre(b)
            normed(b)

        def chunk(c, first):
            for p in range(1, NPE):
                pool.wait_ge(scale_done, c * NPE + p + 1)
                pool.wait_ge(add_done, c * 7 + p - 1)
                if p < NPE - 1:
                    nc.gpsimd.tensor_tensor(acc[:], acc[:], res[p % 2][:], ALU.add).then_inc(add_done, 1)
                else:
                    if not first:
                        pool.wait_ge(y_done, c)
                    nc.gpsimd.tensor_tensor(acc_f[:], acc[:], res[p % 2][:], ALU.add).then_inc(add_done, 1)
                if first and p == 2:
                    centre(NB - 1)
                if first and p == 4:
                    normed(NB - 1)

        chunk(0, True)
        with pool.Fori(1, NCH) as c:
            chunk(c, False)

    @block.scalar
    def _(act):
        def twice(v):
            return v.rearrange("(a p b) -> a p b", a=1, b=1).broadcast_to([2, C, 1])

        halves = (slice(0, C), slice(C, 128))
        act.wait_ge(pool_const, 2)
        for half in halves:
            act.dma_start(wq_bd[half, half], wq_tok).then_inc(tok_loaded, 16)
            act.dma_start(wk_bd[half, half], wk_tok).then_inc(tok_loaded, 16)
        act.dma_start(b_col[:], twice(b_tok)).then_inc(bias_loaded, 16)
        act.dma_start(v_col[:], twice(v_tok)).then_inc(bias_loaded, 16)

        def tokens_out(p):
            act.wait_ge(xt_ps, p + 1)
            act.wait_ge(k_ps, p - 1)
            bank = 6 * (p % 2)
            act.copy(x_t[:, p % 2, 0:BK], ps[:, bank, 0:BK])
            act.copy(x_t[:, p % 2, BK:L], ps[:, bank + 1, 0:L - BK]).then_inc(xt_sb, 1)

        def projected(p):
            act.wait_ge(q_ps, p + 1)
            if p == 0:
                act.wait_ge(bias_loaded, 2 * 16)
            nc.scalar.activation(qb[:, p, 8:8 + NW].rearrange("q (h n) -> q h n", h=2), ps[:, 2:4, 0:HALF],
                                 ACT.Identity, bias=b_col[:]).then_inc(q_sb, 1)
            act.wait_ge(k_ps, p + 1)
            act.copy(kx[:, p, 0:L].rearrange("q (h n) -> q h n", h=2), ps[:, 4:6, 0:L // 2]).then_inc(k_sb, 1)

        def exps(p):
            act.wait_ge(shifted, p + 1)
            nc.scalar.activation(wt[:], wt[:], ACT.Exp).then_inc(exp_done, 1)

        def tanhs(p, i):
            act.wait_ge(sum_done, p * 3 + i + 1)
            v = th[:, p % 2, :].rearrange("q (r n) -> q r n", n=QW)[:, 3 * i:3 * i + 3, 8:8 + NW]
            nc.scalar.activation(v, v, ACT.Tanh).then_inc(tanh_done, 1)

        def scores_out(p):
            act.wait_ge(sc_ps, p + 1)
            if p:
                act.wait_ge(sct_ps, p)
            act.copy(sc_s[:, 0:NW].rearrange("q (h n) -> q h n", h=2), ps[0:96, 0:2, 0:HALF]).then_inc(sc_sb, 1)

        def bands_out(p):
            for b in range(2):
                for k in range(2):
                    n = 4 - k
                    act.wait_ge(bt_ps, p * 4 + 2 * b + k + 1)
                    last = act.copy(band_t[:, 7 * b + 4 * k:7 * b + 4 * k + n, :].rearrange("q t n -> q (t n)"),
                                    ps[0:KW, 4 + 2 * b + k, 0:n * TW])
            last.then_inc(bt_sb, 1)

        def sums_out(p):
            act.wait_ge(h_ps, p + 1)
            act.copy(h_all[:, 2 * p:2 * p + 2, :, :].rearrange("q b t c -> q b (t c)"),
                     ps[0:TW, 4:6, 0:NT * C]).then_inc(h_sb, 1)

        projected(0)
        tokens_out(2)
        projected(1)
        tanhs(0, 0)
        tokens_out(3)
        projected(2)
        tanhs(0, 1)
        projected(3)
        tanhs(0, 2)
        for p in range(NPAIR):
            more = p + 1 < NPAIR
            if p > 0:
                exps(p - 1)
            if more:
                tanhs(p + 1, 0)
            if p > 1:
                sums_out(p - 2)
            if more:
                tanhs(p + 1, 1)
            scores_out(p)
            if p > 0:
                bands_out(p - 1)
            if more:
                tanhs(p + 1, 2)
            if p == 1:
                act.wait_ge(w_loaded, N_W_LOADS * 16)
                act.copy(qw_r[:], qw_f[:]).then_inc(act_const, 1)
                act.copy(gw_r[:, 0, :], gw_f[:]).then_inc(act_const, 1)
        def w_high(k):
            act.copy(w_hi[k][:].rearrange("d e h -> d (e h)"), w_f[k][:]).then_inc(act_const, 1)

        exps(NPAIR - 1)
        def key_hi(b, par, bank=4):
            act.wait_ge(kt_ps, b + 1)
            act.copy(k_hi[par][:, 0:BK], ps[:, bank, 0:BK])
            act.copy(k_hi[par][:, BK:NW], ps[:, bank + 1, 0:NW - BK]).then_inc(khi_sb, 1)

        def query_hi(b, par, bank=4):
            act.wait_ge(qq_ps, b + 1)
            act.copy(q_s[par][:].rearrange("q (h n) -> q h n", h=2), ps[:, bank:bank + 2, 0:NQ]).then_inc(qhi_sb, 1)

        def sigmoid(b, par, j, tail):
            n = (par + j) % 2
            act.wait_ge(s_ps, b * NT + j + 1)
            if j >= 2 or tail:
                act.wait_ge(av_done, b * NT + j - 1)
            nc.scalar.activation(att[n][0:tile_n(j)], ps[0:tile_n(j), 2 * n:2 * n + 2, 0:NQ],
                                 ACT.Sigmoid).then_inc(sig_done, 1)

        def x2_hi(b, bank=4):
            act.wait_ge(x2t_ps, b + 1 + AHEAD)
            act.wait_ge(x3_stored, b * 16 + DMA_AHEAD)
            act.wait_ge(gate_ps, b + AHEAD)
            act.copy(x2_s[:, 0:BK], ps[:, bank, 0:BK])
            act.copy(x2_s[:, BK:NW], ps[:, bank + 1, 0:NW - BK]).then_inc(x2hi_sb, 1)

        def dispatch_weights(g):
            act.wait_ge(routed, g + 1)
            nc.scalar.activation(r_w[:, 0, :], r_m[:, 2, :], ACT.Sigmoid, scale=-1.0)
            nc.scalar.activation(r_w[:, 1, :], r_m[:, 2, :], ACT.Sigmoid).then_inc(rw_ready, 1)

        def dispatch_out(g, bank):
            act.wait_ge(dt_ps, g + 1)
            act.copy(d_t[:, g * GB:(g + 1) * GB, :].rearrange("q b n -> q (b n)"), ps[0:NT * E, bank, 0:BK]
                     ).then_inc(dt_sb, 1)

        def step(b, par, prep, tail, lag):
            sigmoid(b, par, 0, tail)
            sigmoid(b, par, 1, tail)
            if not tail:
                sums_out(NPAIR - 1)
            if not prep:
                dispatch_weights(0)
            if lag:
                x2_hi(b - 2)
            sigmoid(b, par, 2, tail)
            sigmoid(b, par, 3, tail)
            if prep:
                key_hi(b + 1, 1 - par)
            sigmoid(b, par, 4, tail)
            if not prep:
                dispatch_out(0, 4)
            sigmoid(b, par, 5, tail)
            if prep:
                query_hi(b + 1, 1 - par)
            sigmoid(b, par, 6, tail)

        act.wait_ge(sums_read, 1)
        key_hi(0, 0, 0)
        w_high(0)
        sums_out(NPAIR - 2)
        query_hi(0, 0, 0)
        w_high(1)
        bands_out(NPAIR - 1)
        step(0, 0, True, False, False)
        step(1, 1, True, True, False)
        with act.Fori(0, 2) as i:
            step(i * 2 + 2, 0, True, True, True)
            step(i * 2 + 3, 1, True, True, True)
        step(6, 0, True, True, True)
        step(7, 1, False, True, True)

        def silu(c, e, first):
            act.wait_ge(h_ready, c * E + e + 1)
            if not (first and e < 2):
                act.wait_ge(prod_done, c * E + e - 1)
            nc.scalar.activation(sil[e % 2][:], ps[:, e % 2, 0:CH], ACT.Silu).then_inc(sil_done, 1)

        for e in range(E):
            silu(0, e, True)
            if e == 1:
                x2_hi(NB - 2, 6)
        x2_hi(NB - 1, 6)
        with act.Fori(1, 2) as c:
            for e in range(E):
                silu(c, e, False)
        with act.Fori(2, 3) as c:
            for e in range(E):
                silu(c, e, False)
                if e == 11:
                    dispatch_weights(1)
        with act.Fori(3, 4) as c:
            for e in range(E):
                silu(c, e, False)
                if e == 5:
                    dispatch_out(1, 7)
        with act.Fori(4, NCH) as c:
            for e in range(E):
                silu(c, e, False)

    @block.tensor
    def _(pe):
        pe.wait_ge(pool_const, 11)
        def tokens_t(p):
            pe.wait_ge(x_loaded[p], 48)
            if p >= 2:
                pe.wait_ge(xt_first, p - 1)
            for t in range(NT):
                n = TW if t < NT - 1 else L - t * TW
                bank, o = divmod(t, 4)
                last = nc.tensor.transpose(ps[:, 6 * (p % 2) + bank, o * TW:o * TW + n],
                                           xk[0:n, p, t, :, :].rearrange("q b c -> q (b c)"), ident[0:n, 0:n])
            last.then_inc(xt_ps, 1)

        def project_in(p):
            if p == 0:
                pe.wait_ge(tok_loaded, N_TOK_LOADS * 16)
            if p < 2:
                pe.wait_ge(xt_first, p + 1)
            else:
                pe.wait_ge(xt_sb, p - 1)
            if p >= 1:
                pe.wait_ge(q_sb, p)
            for h in range(2):
                last = nc.tensor.matmul(ps[:, 2 + h, 0:HALF], wq_bd[:],
                                        x_t[:, p % 2, 4 + h * HALF:4 + (h + 1) * HALF], start=True, stop=True)
            last.then_inc(q_ps, 1)
            if p >= 1:
                pe.wait_ge(k_sb, p)
            for h in range(2):
                last = nc.tensor.matmul(ps[:, 4 + h, 0:L // 2], wk_bd[:],
                                        x_t[:, p % 2, h * (L // 2):(h + 1) * (L // 2)], start=True, stop=True)
            last.then_inc(k_ps, 1)

        def keep_warm(n, bank=7):
            for _ in range(n):
                nc.tensor.matmul(ps[:, bank, 0:128], ident[:], ident[:], start=True, stop=True)

        keep_warm(9)
        tokens_t(0)
        keep_warm(3)
        project_in(0)
        tokens_t(1)
        for p in range(1, NPAIR):
            if p + 1 < NPAIR:
                tokens_t(p + 1)
            project_in(p)
        pe.wait_ge(q_sb, NPAIR)
        pe.wait_ge(k_sb, NPAIR)

        def token_scores(p, i):
            pe.wait_ge(tanh_done, p * 3 + i + 1)
            if i == 0 and p:
                pe.wait_ge(sc_sb, p)
            src = th[:, p % 2, :].rearrange("q (r n) -> q r n", n=QW)
            for h in range(2):
                for g in range(3):
                    last = nc.tensor.matmul(
                        ps[32 * g:32 * g + 32, h, 0:HALF], v_sel[:, i, :],
                        src[:, 3 * i + g, 8 + h * HALF:8 + (h + 1) * HALF], start=(i == 0), stop=(i == 2))
            if i == 2:
                last.then_inc(sc_ps, 1)

        def scores_t(p):
            pe.wait_ge(sc_sb, p + 1)
            if p:
                pe.wait_ge(wt_copied, p)
            for t in range(NT):
                bank, o = divmod(t, 4)
                last = nc.tensor.transpose(ps[0:TW, 2 + bank, o * 96:o * 96 + 96], sc_s[:, t * TW:(t + 1) * TW],
                                           ident[0:96, 0:96])
            last.then_inc(sct_ps, 1)

        def bands_t(p):
            if p:
                pe.wait_ge(h_sb, p)
            for b in range(2):
                pe.wait_ge(band_ready, 2 * p + b + 1)
                for k in range(2):
                    for t in range(4 * k, min(4 * k + 4, NT)):
                        o = t % 4
                        last = nc.tensor.transpose(ps[0:KW, 4 + 2 * b + k, o * TW:(o + 1) * TW],
                                                   band_a[:, b * NT + t, 0:KW], ident[0:TW, 0:TW])
                    last.then_inc(bt_ps, 1)

        def window_sums(p):
            pe.wait_ge(bt_sb, p + 1)
            for b in range(2):
                for t in range(NT):
                    k = tile_n(t) + WIN - 1
                    last = nc.tensor.matmul(ps[0:TW, 4 + b, t * C:(t + 1) * C], band_t[0:k, b * NT + t, :],
                                            xk[0:k, p, t, b, :], start=True, stop=True)
            last.then_inc(h_ps, 1)

        pe.wait_ge(dve_const, 3)
        for p in range(NPAIR):
            token_scores(p, 0)
            token_scores(p, 1)
            if p > 1:
                window_sums(p - 2)
            token_scores(p, 2)
            if p == NPAIR - 1:
                scores_t(p)
            if p > 0:
                bands_t(p - 1)
            if p < NPAIR - 1:
                scores_t(p)

        def key_t(b, par, lag=False, first=4):
            if lag:
                pe.wait_ge(x2_ready, b - 2)
            pe.wait_ge(xs_loaded, (b + 1) * 32)
            for t in range(NT):
                n = tile_n(t)
                bank, o = divmod(t, 4)
                last = nc.tensor.transpose(ps[:, first + bank, o * TW:o * TW + n],
                                           xs[par][0:n, t, :, :].rearrange("q k c -> q (k c)"), ident[0:n, 0:n])
            last.then_inc(kt_ps, 1)

        def query(b, par, first=4):
            pe.wait_ge(klo_sb, b + 1)
            for h in range(2):
                cols = slice(h * NQ, (h + 1) * NQ)
                nc.tensor.matmul(ps[:, first + h, 0:NQ], qw_r[:], k_hi[par][:, cols], start=True, stop=False)
                last = nc.tensor.matmul(ps[:, first + h, 0:NQ], qw_r[:], k_lo[par][:, cols], start=False, stop=True)
            last.then_inc(qq_ps, 1)

        def scores(b, par, j):
            n = (par + j) % 2
            m = tile_n(j)
            if j == 0:
                pe.wait_ge(qlo_sb, b + 1)
            for h in range(2):
                cols = slice(h * NQ, (h + 1) * NQ)
                for part in (k_hi, k_lo):
                    last = nc.tensor.matmul(ps[0:m, 2 * n + h, 0:NQ], part[par][:, j * TW:j * TW + m],
                                            q_s[par][:, cols], start=part is k_hi, stop=part is k_lo)
            last.then_inc(s_ps, 1)

        def values(b, par, j):
            n = (par + j) % 2
            m = tile_n(j)
            pe.wait_ge(sig_done, b * NT + j + 1)
            if j == 0:
                pe.wait_ge(o_sb, b)
            for h in range(2):
                last = nc.tensor.matmul(ps[h * C:(h + 1) * C, 6, 0:NQ], xs[par][0:m, j, 0, :], att[n][0:m, h, :],
                                        start=(j == 0), stop=(j == NT - 1))
            last.then_inc(av_done, 1)

        def back_waits(b, lag):
            if lag:
                pe.wait_ge(gate_sb, b - 1 + AHEAD)
            pe.wait_ge(o_sb, b + 1)

        def back(b):
            for t in range(NT):
                last = nc.tensor.transpose(ps[0:TW, 7, t * C:(t + 1) * C], o_t[:, t * TW:(t + 1) * TW],
                                           ident[0:C, 0:C])
            last.then_inc(ot_ps, 1)

        def norm_t(b, first=4):
            pe.wait_ge(xn2_ready, b + 1)
            if first == 6:
                pe.wait_ge(o_sb, NB)
                pe.wait_ge(gate_sb, b + AHEAD)
            for t in range(NT):
                n = tile_n(t)
                bank, o = divmod(t, 4)
                last = nc.tensor.transpose(ps[:, first + bank, o * TW:o * TW + n],
                                           xn2[0:n, t, :, :].rearrange("q k c -> q (k c)"), ident[0:n, 0:n])
            last.then_inc(x2t_ps, 1)

        def gates(b, lag=False):
            if lag:
                pe.wait_ge(h2_ready, b + 2)
            pe.wait_ge(x2_ready, b + 1)
            for t in range(NT):
                last = nc.tensor.matmul(ps[0:TW, 7, t * 2 * E:(t + 1) * 2 * E], x2_s[:, t * TW:(t + 1) * TW],
                                        gw_r[:].rearrange("d k e -> d (k e)"), start=True, stop=True)
            last.then_inc(gate_ps, 1)

        def dispatch_t(g, bank):
            pe.wait_ge(disp_ready, g + 1)
            for b in range(GB):
                last = nc.tensor.transpose(ps[0:NT * E, bank, b * TW:(b + 1) * TW],
                                           logit[:, g * GB + b, :, :].rearrange("q t e -> q (t e)"),
                                           ident[0:TW, 0:TW])
            last.then_inc(dt_ps, 1)

        def step(b, par, prep, tail, lag):
            if tail:
                scores(b, par, 0)
                scores(b, par, 1)
            if lag:
                norm_t(b - 2)
            values(b, par, 0)
            if tail:
                back_waits(b - 1, lag)
            scores(b, par, 2)
            if tail:
                back(b - 1)
            values(b, par, 1)
            scores(b, par, 3)
            if not tail:
                pe.wait_ge(h_sb, NPAIR)
            if prep:
                key_t(b + 1, 1 - par, lag)
            values(b, par, 2)
            scores(b, par, 4)
            if not prep:
                pe.wait_ge(x2_ready, NB - 2)
                dispatch_t(0, 4)
            values(b, par, 3)
            scores(b, par, 5)
            if prep:
                query(b + 1, 1 - par)
            values(b, par, 4)
            scores(b, par, 6)
            if lag:
                gates(b - 2, True)
            values(b, par, 5)
            values(b, par, 6)

        key_t(0, 0, first=0)
        window_sums(NPAIR - 2)
        pe.wait_ge(dve_const, 4)
        query(0, 0, 0)
        scores(0, 0, 0)
        scores(0, 0, 1)
        bands_t(NPAIR - 1)
        window_sums(NPAIR - 1)
        step(0, 0, True, False, False)
        step(1, 1, True, True, False)
        with pe.Fori(0, 2) as i:
            step(i * 2 + 2, 0, True, True, True)
            step(i * 2 + 3, 1, True, True, True)
        step(6, 0, True, True, True)
        step(7, 1, False, True, True)

        pe.wait_ge(w_split, 1)
        def expert(c, e, first):
            k = e % 2
            if not (first and e < 2):
                pe.wait_ge(prod_done, c * E + e - 1)
            xc = x3[:, bass.ds(c * CH, CH)]
            for j in range(2):
                nc.tensor.matmul(ps[:, 2 * j + k, 0:CH], w_hi[j][:, e, :], xc, start=True, stop=False)
                last = nc.tensor.matmul(ps[:, 2 * j + k, 0:CH], w_lo[j][:, e, :], xc, start=False, stop=True)
            last.then_inc(h_ready, 1)

        def project(c, p, first):
            pe.wait_ge(prod_done, c * E + 2 * p + 2)
            if not (first and p < 2):
                pe.wait_ge(scale_done, c * NPE + p - 1)
            for k in range(2):
                e = 2 * p + k
                last = nc.tensor.matmul(ps[k * C:(k + 1) * C, 4 + p % 2, 0:CH], w3_s[:, e, :], prod[e % 4][:],
                                        start=True, stop=True)
            last.then_inc(out_done, 1)

        def collect(c):
            pe.wait_ge(add_done, c * 7 + 7)
            pe.wait_ge(fin_done, c + AHEAD)
            for j in range(4):
                last = nc.tensor.matmul(ps[0:YT, 6, j * C:(j + 1) * C], acc_f[:, j * YT:(j + 1) * YT], stack2[:],
                                        start=True, stop=True)
            last.then_inc(y_done, 1)

        def chunk(c, first=False, late=0):
            for p in range(NPE):
                expert(c, 2 * p, first)
                expert(c, 2 * p + 1, first)
                if first and p == 0:
                    norm_t(NB - 2, 6)
                if first and p == 1:
                    pe.wait_ge(dt_sb, 1)
                if first and p == 2:
                    gates(NB - 2)
                if first and p == 3:
                    back_waits(NB - 1, False)
                    pe.wait_ge(gate_sb, NB - 1 + AHEAD)
                    back(NB - 1)
                if late == 1 and p == 1:
                    gates(NB - 1)
                if late == 2 and p == 1:
                    dispatch_t(1, 7)
                if p > 0:
                    project(c, p - 1, first)
                elif not first:
                    project(c - 1, NPE - 1, False)
                if p == 2 and not first:
                    collect(c - 1)

        chunk(0, first=True)
        norm_t(NB - 1, 6)
        with pe.Fori(1, 2) as c:
            chunk(c, late=1)
        with pe.Fori(2, 3) as c:
            chunk(c)
        with pe.Fori(3, 4) as c:
            chunk(c, late=2)
        with pe.Fori(4, C_HALF) as c:
            chunk(c)
        pe.wait_ge(x3_stored, NB * 16 + DMA_AHEAD)
        with pe.Fori(C_HALF, NCH) as c:
            chunk(c)
        project(NCH - 1, NPE - 1, False)
        collect(NCH - 1)

    @block.vector
    def _(dve):
        class Chain:

            def __init__(self, base):
                self.base, self.n = base, 0

            def link(self, ins):
                self.n += 1
                ins.then_inc(dve_step, 1)
                dve.wait_ge(dve_step, self.base + self.n)

        tt, ts = nc.vector.tensor_tensor, nc.vector.tensor_scalar

        nc.vector.memset(qb[:, :, 0:8], 0.0)
        nc.vector.memset(qb[:, :, 8 + NW:QW], 0.0)
        nc.vector.memset(kx[:, :, L:KXW], 0.0)
        nc.vector.memset(sc_s[:, NW:NWP], 0.0)
        nc.vector.memset(v_sel[:], 0.0).then_inc(dve_const, 1)
        for e in range(E):
            last = nc.vector.memset(rank[:, e:e + 1], float(E - e))
        last.then_inc(dve_const, 1)
        for p in range(2):
            dve.wait_ge(xt_ps, p + 1)
            nc.vector.tensor_copy(x_t[:, p, 0:BK], ps[:, 6 * p, 0:BK])
            nc.vector.tensor_copy(x_t[:, p, BK:L], ps[:, 6 * p + 1, 0:L - BK]).then_inc(xt_first, 1)
        dve.wait_ge(dve_const, 2)
        dve.wait_ge(bias_loaded, 2 * 16)
        for k in range(2):
            for i in range(3):
                last = nc.vector.tensor_copy(v_sel[k * C:(k + 1) * C, i, 3 * k + i:3 * k + i + 1],
                                             v_col[k * C:(k + 1) * C, :])
        last.then_inc(dve_const, 1)
        def sums(p, i):
            if i == 0:
                dve.wait_ge(q_sb, p + 1)
                dve.wait_ge(k_sb, p + 1)
            for g in range(3):
                r, o = 3 * g + i, (3 * i + g) * QW
                dst = th[:, p % 2, o + r:o + r + KXW].rearrange("q (s w) -> q s w", w=WIN)
                q = qb[:, p, r:r + KXW].rearrange("q (s w) -> q s w", w=WIN)
                k = kx[:, p, :].rearrange("q (s w) -> q s w", w=WIN)[:, :, r:r + 1]
                last = tt(dst, q, k.broadcast_to([128, SEG, WIN]), ALU.add)
            last.then_inc(sum_done, 1)

        def softmax_top(p):
            dve.wait_ge(sct_ps, p + 1)
            if p:
                dve.wait_ge(band_ready, 2 * p)
            for b in range(2):
                for k in range(2):
                    n = 4 - k
                    src = ps[0:TW, 2 + k, 0:n * 96].rearrange("q (t g i) -> q t g i", t=n, g=3)
                    last = nc.vector.tensor_copy(
                        wt[:, b, 4 * k:4 * k + n, :].rearrange("q t (g i) -> q t g i", g=3),
                        src[:, :, :, 3 * b:3 * b + 3])
            last.then_inc(wt_copied, 1)
            dve.wait_ge(wt_copied, p + 1)
            chain.link(nc.vector.tensor_reduce(wt_max[:], wt_rows, AX.X, ALU.max))
            tt(wt_rows, wt_rows, wt_max[:].unsqueeze(2).broadcast_to([TW, 2 * NT, WIN]), ALU.subtract
               ).then_inc(shifted, 1)

        def softmax_end(p):
            dve.wait_ge(exp_done, p + 1)
            chain.link(nc.vector.tensor_reduce(wt_sum[:], wt_rows, AX.X, ALU.add))
            chain.link(nc.vector.reciprocal(wt_sum[:], wt_sum[:]))
            tt(wt_rows, wt_rows, wt_sum[:].unsqueeze(2).broadcast_to([TW, 2 * NT, WIN]), ALU.mult
               ).then_inc(wt_ready, 1)

        def mean_a(p):
            dve.wait_ge(h_sb, p + 1)
            h = h_all[:, 2 * p:2 * p + 2, :, :].rearrange("q b t c -> q (b t) c")
            chain.link(nc.vector.tensor_reduce(ln_s[:, p % 2, 1, :], h, AX.X, ALU.add))
            ts(ln_s[:, p % 2, 0, :], ln_s[:, p % 2, 1, :], 1.0 / C, None, ALU.mult).then_inc(mean_ready, 1)

        def var_a(p):
            dve.wait_ge(sq_ready, p + 1)
            chain.link(nc.vector.tensor_reduce(ln_s[:, p % 2, 1, :], ln_sq[:], AX.X, ALU.add))
            ts(ln_s[:, p % 2, 2, :], ln_s[:, p % 2, 1, :], 1.0 / C, 1e-5, ALU.mult, ALU.add).then_inc(var_ready, 1)

        def normed_a(p):
            dve.wait_ge(rstd_ready, p + 1)
            tt(xn_all[:, 2 * p:2 * p + 2, :, :].rearrange("q b t c -> q (b t) c"), ln_c[:],
               ln_s[:, p % 2, 3, :].unsqueeze(2).broadcast_to([TW, 2 * NT, C]), ALU.mult).then_inc(xn_ready, 1)

        wt_rows = wt[:].rearrange("q b t r -> q (b t) r")
        chain = Chain(0)
        for i in range(3):
            sums(0, i)
        for p in range(NPAIR):
            more = p + 1 < NPAIR
            if more and p > 0:
                dve.wait_ge(sc_ps, p)
            if more:
                sums(p + 1, 0)
            if p > 0:
                softmax_top(p - 1)
                if not more:
                    var_a(0)
                softmax_end(p - 1)
            if more:
                sums(p + 1, 1)
            if p == 2:
                mean_a(0)
            if more:
                sums(p + 1, 2)
            if p == NPAIR - 2:
                dve.wait_ge(act_const, 2)
                tt(qw_r[C:128, :], qw_f[C:128, :], qw_r[C:128, :].bitcast(F32), ALU.subtract)
                tt(gw_r[:, 1, :], gw_f[:], gw_r[:, 0, :].bitcast(F32), ALU.subtract).then_inc(dve_const, 1)
                dve.wait_ge(sum_done, NPAIR * 3)
                for par in range(2):
                    nc.vector.memset(k_hi[par][:, NW:NWP].bitcast(F32), 0.0)
                    last = nc.vector.memset(k_lo[par][:, NW:NWP].bitcast(F32), 0.0)
                last.then_inc(sums_read, 1)
        normed_a(0)
        softmax_top(NPAIR - 1)
        softmax_end(NPAIR - 1)

        def pads():
            nc.vector.memset(x2_s[:, NW:NWP].bitcast(F32), 0.0)
            nc.vector.memset(x3[:, TOK:TOKP].bitcast(F32), 0.0)
            nc.vector.memset(zrow[:], 0.0)
            nc.vector.memset(o_t[:, NW:NWP], 0.0).then_inc(b_init, 1)

        def key_lo(b, par, bank=4):
            dve.wait_ge(khi_sb, b + 1)
            tt(k_lo[par][:, 0:BK], ps[:, bank, 0:BK], k_hi[par][:, 0:BK].bitcast(F32), ALU.subtract)
            tt(k_lo[par][:, BK:NW], ps[:, bank + 1, 0:NW - BK], k_hi[par][:, BK:NW].bitcast(F32), ALU.subtract
               ).then_inc(klo_sb, 1)

        def query_lo(b, par, bank=4):
            dve.wait_ge(qhi_sb, b + 1)
            low = q_s[par][C:128, :].rearrange("q (h n) -> q h n", h=2)
            tt(low, ps[C:128, bank:bank + 2, 0:NQ], low.bitcast(F32), ALU.subtract).then_inc(qlo_sb, 1)

        def attended(b):
            dve.wait_ge(av_done, (b + 1) * NT)
            dve.wait_ge(ot_ps, b + AHEAD)
            nc.vector.tensor_copy(o_t[:, 0:NQ], ps[0:C, 6, 0:NQ])
            nc.vector.tensor_copy(o_t[:, NQ:NW], ps[C:128, 6, 0:NW - NQ]).then_inc(o_sb, 1)

        def residual(b, chain):
            dve.wait_ge(ot_ps, b + 1 + AHEAD)
            dve.wait_ge(h2_stored, b * 32 + DMA_AHEAD)
            tt(h2_s[:], ps[0:TW, 7, 0:NT * C].rearrange("q (t c) -> q t c", c=C),
               h_all[:, bass.ds(b, 1), :, :].rearrange("q a t c -> q (a t) c"), ALU.add).then_inc(h2_ready, 1)
            dve.wait_ge(h2_ready, b + 1)
            chain.link(nc.vector.tensor_reduce(bn_s[:, 1, :], h2_s[:], AX.X, ALU.add))
            ts(bn_s[:, 0, :], bn_s[:, 1, :], 1.0 / C, None, ALU.mult).then_inc(mean2, 1)

        def variance(b, chain):
            dve.wait_ge(sq2, b + 1)
            chain.link(nc.vector.tensor_reduce(bn_s[:, 1, :], bn_sq[:], AX.X, ALU.add))
            ts(bn_s[:, 2, :], bn_s[:, 1, :], 1.0 / C, 1e-5, ALU.mult, ALU.add).then_inc(var2, 1)

        def x2_lo(b, bank=4):
            dve.wait_ge(x2hi_sb, b + 1)
            tt(x2_s[C:128, 0:BK], ps[C:128, bank, 0:BK], x2_s[C:128, 0:BK].bitcast(F32), ALU.subtract)
            tt(x2_s[C:128, BK:NW], ps[C:128, bank + 1, 0:NW - BK], x2_s[C:128, BK:NW].bitcast(F32), ALU.subtract
               ).then_inc(x2_ready, 1)

        def logits(b, chain):
            lg = logit[:, bass.ds(b, 1), :, :].rearrange("q a t e -> q (a t) e")
            dve.wait_ge(gate_ps, b + 1 + AHEAD)
            parts = ps[0:TW, 7, 0:NT * 2 * E].rearrange("q (t k e) -> q k t e", k=2, e=E)
            chain.link(tt(lg, parts[:, 0], gb_row[:].unsqueeze(1).broadcast_to([TW, NT, E]), ALU.add))
            tt(lg, parts[:, 1], lg, ALU.add).then_inc(gate_sb, 1)

        ROUTE_PARTS, DISPATCH_PARTS = 11, 3

        def route(g, part, chain):
            over = lambda v: v.unsqueeze(2).broadcast_to([TW, GB * NT, E])
            lg = logit[:, g * GB:(g + 1) * GB, :, :].rearrange("q b t e -> q (b t) e")
            rk = rank[:].unsqueeze(1).broadcast_to([TW, GB * NT, E])
            if part == 0:
                chain.link(nc.vector.tensor_reduce(r_m[:, 0, :], lg, AX.X, ALU.max))
            elif part == 1:
                chain.link(tt(lg, lg, over(r_m[:, 0, :]), ALU.subtract))
            elif part == 2:
                chain.link(nc.vector.scalar_tensor_tensor(r_b[:], lg, 0.0, rk, ALU.is_equal, ALU.mult))
            elif part == 3:
                chain.link(nc.vector.tensor_reduce(r_m[:, 1, :], r_b[:], AX.X, ALU.max))
            elif part == 4:
                chain.link(tt(r_b[:], r_b[:], over(r_m[:, 1, :]), ALU.is_equal))
            elif part == 5:
                chain.link(nc.vector.scalar_tensor_tensor(r_a[:], r_b[:], -BIG, lg, ALU.mult, ALU.add))
            elif part == 6:
                chain.link(nc.vector.tensor_reduce(r_m[:, 2, :], r_a[:], AX.X, ALU.max))
            elif part == 7:
                chain.link(tt(r_a[:], r_a[:], over(r_m[:, 2, :]), ALU.is_equal))
            elif part == 8:
                chain.link(tt(r_a[:], r_a[:], rk, ALU.mult))
            elif part == 9:
                chain.link(nc.vector.tensor_reduce(r_m[:, 3, :], r_a[:], AX.X, ALU.max))
            else:
                tt(r_a[:], r_a[:], over(r_m[:, 3, :]), ALU.is_equal).then_inc(routed, 1)

        def dispatch(g, part, chain):
            over = lambda v: v.unsqueeze(2).broadcast_to([TW, GB * NT, E])
            if part == 0:
                dve.wait_ge(rw_ready, g + 1)
                dve.wait_ge(routed, g + 1)
                tt(r_b[:], r_b[:], over(r_w[:, 0, :]), ALU.mult)
            elif part == 1:
                chain.link(tt(r_a[:], r_a[:], over(r_w[:, 1, :]), ALU.mult))
            else:
                tt(logit[:, g * GB:(g + 1) * GB, :, :].rearrange("q b t e -> q (b t) e"), r_b[:], r_a[:], ALU.add
                   ).then_inc(disp_ready, 1)

        TAIL_LINKS, B_LINKS = 2, 3
        b_first = NPAIR * 5

        def step(b, par, prep, tail, lag, chain=None):
            if chain is None:
                chain = Chain((b - 2) * B_LINKS + b_first + TAIL_LINKS)
                routing = False
            else:
                routing = True
            if tail:
                attended(b - 1)
            if routing and not prep:
                for part in range(9, ROUTE_PARTS):
                    route(0, part, chain)
            if lag:
                x2_lo(b - 2)
            if routing and not prep:
                for part in range(DISPATCH_PARTS):
                    dispatch(0, part, chain)
            if tail:
                residual(b - 1, chain)
            if routing and prep:
                dve.wait_ge(gate_sb, GB + AHEAD)
                for part in range(0, 3):
                    route(0, part, chain)
            if prep:
                key_lo(b + 1, 1 - par)
            if tail:
                variance(b - 1, chain)
            if routing and prep:
                for part in range(3, 6):
                    route(0, part, chain)
            if prep:
                query_lo(b + 1, 1 - par)
            if lag:
                logits(b - 2, chain)
            if routing and prep:
                for part in range(6, 9):
                    route(0, part, chain)

        def w_low(k):
            dve.wait_ge(act_const, 3 + k)
            return tt(w_lo[k][:].rearrange("d e h -> d (e h)"), w_f[k][:],
                      w_hi[k][:].rearrange("d e h -> d (e h)").bitcast(F32), ALU.subtract)

        key_lo(0, 0, 0)
        query_lo(0, 0, 0)
        mean_a(1)
        mean_a(2)
        w_low(0)
        w_low(1).then_inc(w_split, 1)
        var_a(1)
        normed_a(1)
        mean_a(NPAIR - 1)
        dve.wait_ge(h_sb, NPAIR)
        pads()
        key_lo(1, 1)
        query_lo(1, 1)
        var_a(2)
        attended(0)
        normed_a(2)
        residual(0, chain)
        key_lo(2, 0)
        var_a(NPAIR - 1)
        variance(0, chain)
        query_lo(2, 0)
        assert chain.n == b_first + TAIL_LINKS
        with dve.Fori(0, 2) as i:
            step(i * 2 + 2, 0, True, True, True)
            step(i * 2 + 3, 1, True, True, True)
        chain = Chain(b_first + TAIL_LINKS + 4 * B_LINKS)
        step(6, 0, True, True, True, chain)
        step(7, 1, False, True, True, chain)
        attended(NB - 1)

        def product(c, e, first):
            dve.wait_ge(sil_done, c * E + e + 1)
            if not (first and e < 4):
                dve.wait_ge(out_done, c * NPE + e // 2 - 1)
            tt(prod[e % 4][:], sil[e % 2][:], ps[:, 2 + e % 2, 0:CH], ALU.mult).then_inc(prod_done, 1)

        def scale(c, p, first):
            dve.wait_ge(out_done, c * NPE + p + 1)
            dve.wait_ge(db_loaded[p % 4], (c * 2 + p // 4 + 1) * 16)
            if p >= 3:
                dve.wait_ge(add_done, c * 7 + p - 2)
            elif not first:
                dve.wait_ge(add_done, c * 7)
            dst = acc if p == 0 else res[p % 2]
            tt(dst[:], ps[:, 4 + p % 2, 0:CH], db[p % 4][:], ALU.mult).then_inc(scale_done, 1)

        def finish(c, first):
            dve.wait_ge(y_done, c + 1)
            dve.wait_ge(h2_loaded, (c + 1) * 16)
            if not first:
                dve.wait_ge(out_stored, c * 16 + DMA_AHEAD)
            tt(fin[:], ps[0:YT, 6, 0:4 * C].rearrange("q (j c) -> q j c", c=C), h2_c[:], ALU.add
               ).then_inc(fin_done, 1)

        def chunk(c, first=False, late=False):
            for p in range(NPE):
                product(c, 2 * p, first)
                product(c, 2 * p + 1, first)
                if p > 0:
                    scale(c, p - 1, first)
                elif not first:
                    scale(c - 1, NPE - 1, False)
                if first and p == 1:
                    x2_lo(NB - 2, 6)
                if first and p == 2:
                    logits(NB - 2, chain)
                if first and p == 3:
                    residual(NB - 1, chain)
                if first and p == 5:
                    variance(NB - 1, chain)
                if late and c == 1 and p == 0:
                    x2_lo(NB - 1, 6)
                if late and c == 1 and p == 1:
                    logits(NB - 1, chain)
                    dve.wait_ge(gate_sb, NB + AHEAD)
                turn = c * NPE + p - (NPE + 2) if late else -1
                if 0 <= turn < ROUTE_PARTS:
                    route(1, turn, chain)
                elif 0 <= turn - ROUTE_PARTS - 1 < DISPATCH_PARTS:
                    dispatch(1, turn - ROUTE_PARTS - 1, chain)
                if p == 3 and not first:
                    finish(c - 1, False)

        chunk(0, first=True)
        for c in range(1, 4):
            chunk(c, late=True)
        with dve.Fori(4, NCH) as c:
            chunk(c)
        scale(NCH - 1, NPE - 1, False)
        finish(NCH - 1, False)

    ctx.close()


_INS = ["x", "L0_tok_W_qry", "L0_tok_W_key", "L0_tok_v", "L0_tok_b", "L0_attn_q_weight", "L0_ffn_gate_w",
        "L0_ffn_gate_b", "L0_ffn_w1", "L0_ffn_w2", "L0_ffn_w3"]


def kernel(**inputs):
    import numpy as _np
    import concourse.bacc as _bacc
    from concourse import mybir as _mybir
    from concourse.bass_utils import run_bass_kernel_spmd as _run

    nc = _bacc.Bacc("TRN2", target_bir_lowering=False, num_devices=1)
    arrays, args = {}, []
    for name in _INS:
        a = _np.ascontiguousarray(inputs[name])
        arrays[f"in_{name}"] = a
        args.append(nc.dram_tensor(f"in_{name}", a.shape, _mybir.dt.from_np(a.dtype), kind="ExternalInput").ap())
    out = nc.dram_tensor("out_0", (NB, NW, C), _mybir.dt.float32, kind="ExternalOutput").ap()
    build(nc, *args, out)
    r = _run(nc, [arrays], core_ids=[0])
    return r.results[0]["out_0"]
```
